# Optimizing a Trainium2 kernel written in Bass

```python
import numpy as np
import jax
import jax.numpy as jnp

def _softmax(x, axis=-1):
    return jax.nn.softmax(x, axis=axis)

def _gelu(x):
    return jax.nn.gelu(x, approximate=True)

def _silu(x):
    return jax.nn.silu(x)

def _sigmoid(x):
    return jax.nn.sigmoid(x)

def _layernorm(x, axis=-1, eps=1e-05):
    m = jnp.mean(x, axis=axis, keepdims=True)
    v = jnp.var(x, axis=axis, keepdims=True)
    return (x - m) / jnp.sqrt(v + eps)

def _scatter_add(tgt, idx, src, axis=0):
    return tgt.at[idx].add(src)

def _segment_sum(src, seg, n):
    return jax.ops.segment_sum(src, seg, n)
kernel_name = 'mk_seq_postln_d1_jaxref_r8_cd451e'

def setup_inputs(seed: int=0):
    np.random.seed(seed)
    _w = jnp.asarray

    def _L0_attn_setup():
        import jax, jax.numpy as jnp
        import numpy as np
        import math
        D_K = 64
        key = jax.random.key(seed)
        ks = jax.random.split(key, 5)
        b, m, d, h, dk, dv = (8, 128, 128, 16, 64, 64)
        return {'x': jax.random.normal(ks[0], (b, m, d), dtype=jnp.float32), 'P_q': jax.random.normal(ks[1], (h, d, dk), dtype=jnp.float32) * 0.02, 'P_k': jax.random.normal(ks[2], (h, d, dk), dtype=jnp.float32) * 0.02, 'P_v': jax.random.normal(ks[3], (h, d, dv), dtype=jnp.float32) * 0.02, 'P_o': jax.random.normal(ks[4], (h, d, dv), dtype=jnp.float32) * 0.02}
    _L0_attn_in = _L0_attn_setup()

    def _L0_ffn_setup():
        import jax, jax.numpy as jnp
        import numpy as np
        DIM = 128
        DEPTH = 6
        HEADS = 16
        DIM_HEAD = 64
        WINDOW = 32
        INNER = HEADS * DIM_HEAD
        DIM_INNER = int(DIM * 4 * 2 / 3)
        QK_SCALE = 8.0

        def shift_tokens(t):
            a, s = jnp.split(t, 2, -1)
            s = jnp.pad(s, ((0, 0), (1, 0), (0, 0)))[:, :-1]
            return jnp.concatenate([a, s], -1)

        def l2norm(t):
            return t / jnp.maximum(jnp.linalg.norm(t, axis=-1, keepdims=True), 1e-12)

        def rotate_half(x):
            x1, x2 = jnp.split(x, 2, -1)
            return jnp.concatenate([-x2, x1], -1)

        def rotary_tables(n):
            half = jnp.arange(0, DIM_HEAD, 2, dtype=jnp.float32)
            inv_freq = 1.0 / 10000.0 ** (half / DIM_HEAD)
            t = jnp.arange(n, dtype=jnp.float32)
            freqs = t[:, None] * inv_freq[None, :]
            freqs = jnp.concatenate([freqs, freqs], -1)
            base_scale = (half + 0.4 * DIM_HEAD) / (1.4 * DIM_HEAD)
            power = (t - n // 2) / (WINDOW // 2)
            scale = base_scale[None, :] ** power[:, None]
            scale = jnp.concatenate([scale, scale], -1)
            return (freqs, scale)

        def local_attention(q, k, v):
            b, h, n, d = q.shape
            w = WINDOW
            nw = n // w
            bq = q.reshape(b, h, nw, w, d)
            bk = k.reshape(b, h, nw, w, d)
            bv = v.reshape(b, h, nw, w, d)

            def look(t):
                p = jnp.pad(t, ((0, 0), (0, 0), (1, 0), (0, 0), (0, 0)))
                return jnp.concatenate([p[:, :, :nw], p[:, :, 1:]], axis=3)
            bk2, bv2 = (look(bk), look(bv))
            seq = jnp.arange(n).reshape(nw, w)
            seq_p = jnp.pad(seq, ((1, 0), (0, 0)), constant_values=-1)
            jt = jnp.concatenate([seq_p[:nw], seq_p[1:]], axis=1)
            it = seq[:, :, None]
            jb = jt[:, None, :]
            mask = (it < jb) | (it > jb + w) | (jb == -1)
            sim = jnp.einsum('bhwie,bhwje->bhwij', bq, bk2) * QK_SCALE
            sim = jnp.where(mask, -jnp.finfo(sim.dtype).max, sim)
            attn = jax.nn.softmax(sim, -1)
            out = jnp.einsum('bhwij,bhwje->bhwie', attn, bv2)
            return out.reshape(b, h, n, d)

        def attn_layer(x, Wqkv, qs, ksc, Wo):
            b, n, _ = x.shape
            qkv = x @ Wqkv
            q, k, v = jnp.split(qkv, 3, -1)
            sh = lambda t: t.reshape(b, n, HEADS, DIM_HEAD).transpose(0, 2, 1, 3)
            q, k, v = (sh(q), sh(k), sh(v))
            q = l2norm(q) * qs
            k = l2norm(k) * ksc
            freqs, scale = rotary_tables(n)
            cos, sin = (jnp.cos(freqs), jnp.sin(freqs))
            q = q * cos * scale + rotate_half(q) * sin * scale
            inv = 1.0 / scale
            k = k * cos * inv + rotate_half(k) * sin * inv
            out = local_attention(q, k, v)
            out = out.transpose(0, 2, 1, 3).reshape(b, n, INNER)
            return out @ Wo

        def ffn_layer(x, g, bln, W1, b1, W2, b2):
            mu = x.mean(-1, keepdims=True)
            var = ((x - mu) ** 2).mean(-1, keepdims=True)
            xn = (x - mu) / jnp.sqrt(var + 1e-05) * g + bln
            hg = xn @ W1 + b1
            a, gate = jnp.split(hg, 2, -1)
            return a * jax.nn.gelu(gate, approximate=False) @ W2 + b2
        key = jax.random.key(seed)
        ks = jax.random.split(key, 8)
        B, N = (2, 256)
        init = lambda k, shape: jax.random.normal(k, shape, jnp.float32) * 0.02
        return {'x': jax.random.normal(ks[0], (B, N, DIM), jnp.float32), 'Wqkv': init(ks[1], (DEPTH, DIM, 3 * INNER)), 'q_scale': jnp.ones((DEPTH, DIM_HEAD), jnp.float32), 'k_scale': jnp.ones((DEPTH, DIM_HEAD), jnp.float32), 'Wo': init(ks[2], (DEPTH, INNER, DIM)), 'ln_g': jnp.ones((DEPTH, DIM), jnp.float32), 'ln_b': jnp.zeros((DEPTH, DIM), jnp.float32), 'W1': init(ks[3], (DEPTH, DIM, 2 * DIM_INNER)), 'b1': jnp.zeros((DEPTH, 2 * DIM_INNER), jnp.float32), 'W2': init(ks[4], (DEPTH, DIM_INNER, DIM)), 'b2': jnp.zeros((DEPTH, DIM), jnp.float32)}
    _L0_ffn_in = _L0_ffn_setup()
    _d = {'L0_attn_x': _L0_attn_in['x'], 'L0_attn_P_q': _L0_attn_in['P_q'], 'L0_attn_P_k': _L0_attn_in['P_k'], 'L0_attn_P_v': _L0_attn_in['P_v'], 'L0_attn_P_o': _L0_attn_in['P_o'], 'L0_ffn_Wqkv': _L0_ffn_in['Wqkv'], 'L0_ffn_q_scale': _L0_ffn_in['q_scale'], 'L0_ffn_k_scale': _L0_ffn_in['k_scale'], 'L0_ffn_Wo': _L0_ffn_in['Wo'], 'L0_ffn_ln_g': _L0_ffn_in['ln_g'], 'L0_ffn_ln_b': _L0_ffn_in['ln_b'], 'L0_ffn_W1': _L0_ffn_in['W1'], 'L0_ffn_b1': _L0_ffn_in['b1'], 'L0_ffn_W2': _L0_ffn_in['W2'], 'L0_ffn_b2': _L0_ffn_in['b2']}
    _x0 = _d['L0_attn_x']
    _d['L0_attn_x'] = jax.random.normal(jax.random.fold_in(jax.random.key(seed), 1), (8, 512, 128), dtype=_x0.dtype)
    del _x0
    return _d

def reference(L0_attn_x, L0_attn_P_q, L0_attn_P_k, L0_attn_P_v, L0_attn_P_o, L0_ffn_Wqkv, L0_ffn_q_scale, L0_ffn_k_scale, L0_ffn_Wo, L0_ffn_ln_g, L0_ffn_ln_b, L0_ffn_W1, L0_ffn_b1, L0_ffn_W2, L0_ffn_b2):

    def _L0_attn_ref(x, P_q, P_k, P_v, P_o):
        import jax, jax.numpy as jnp
        import numpy as np
        import math
        D_K = 64
        m = x.shape[1]
        Q = jnp.einsum('bmd,hdk->bhmk', x, P_q)
        K = jnp.einsum('bmd,hdk->bhmk', x, P_k)
        V = jnp.einsum('bmd,hdv->bhmv', x, P_v)
        logits = jnp.einsum('bhmk,bhnk->bhmn', Q, K) * math.sqrt(D_K)
        causal = jnp.tril(jnp.ones((m, m), dtype=bool))
        logits = jnp.where(causal[None, None], logits, -jnp.inf)
        key_weights = jax.nn.softmax(logits, axis=-1)
        o = jnp.einsum('bhmm,bhmv->bhmv', key_weights, V)
        y = jnp.einsum('bhmv,hdv->bmd', o, P_o)
        return y

    def _L0_ffn_ref(x, Wqkv, q_scale, k_scale, Wo, ln_g, ln_b, W1, b1, W2, b2):
        import jax, jax.numpy as jnp
        import numpy as np
        DIM = 128
        DEPTH = 6
        HEADS = 16
        DIM_HEAD = 64
        WINDOW = 32
        INNER = HEADS * DIM_HEAD
        DIM_INNER = int(DIM * 4 * 2 / 3)
        QK_SCALE = 8.0

        def shift_tokens(t):
            a, s = jnp.split(t, 2, -1)
            s = jnp.pad(s, ((0, 0), (1, 0), (0, 0)))[:, :-1]
            return jnp.concatenate([a, s], -1)

        def l2norm(t):
            return t / jnp.maximum(jnp.linalg.norm(t, axis=-1, keepdims=True), 1e-12)

        def rotate_half(x):
            x1, x2 = jnp.split(x, 2, -1)
            return jnp.concatenate([-x2, x1], -1)

        def rotary_tables(n):
            half = jnp.arange(0, DIM_HEAD, 2, dtype=jnp.float32)
            inv_freq = 1.0 / 10000.0 ** (half / DIM_HEAD)
            t = jnp.arange(n, dtype=jnp.float32)
            freqs = t[:, None] * inv_freq[None, :]
            freqs = jnp.concatenate([freqs, freqs], -1)
            base_scale = (half + 0.4 * DIM_HEAD) / (1.4 * DIM_HEAD)
            power = (t - n // 2) / (WINDOW // 2)
            scale = base_scale[None, :] ** power[:, None]
            scale = jnp.concatenate([scale, scale], -1)
            return (freqs, scale)

        def local_attention(q, k, v):
            b, h, n, d = q.shape
            w = WINDOW
            nw = n // w
            bq = q.reshape(b, h, nw, w, d)
            bk = k.reshape(b, h, nw, w, d)
            bv = v.reshape(b, h, nw, w, d)

            def look(t):
                p = jnp.pad(t, ((0, 0), (0, 0), (1, 0), (0, 0), (0, 0)))
                return jnp.concatenate([p[:, :, :nw], p[:, :, 1:]], axis=3)
            bk2, bv2 = (look(bk), look(bv))
            seq = jnp.arange(n).reshape(nw, w)
            seq_p = jnp.pad(seq, ((1, 0), (0, 0)), constant_values=-1)
            jt = jnp.concatenate([seq_p[:nw], seq_p[1:]], axis=1)
            it = seq[:, :, None]
            jb = jt[:, None, :]
            mask = (it < jb) | (it > jb + w) | (jb == -1)
            sim = jnp.einsum('bhwie,bhwje->bhwij', bq, bk2) * QK_SCALE
            sim = jnp.where(mask, -jnp.finfo(sim.dtype).max, sim)
            attn = jax.nn.softmax(sim, -1)
            out = jnp.einsum('bhwij,bhwje->bhwie', attn, bv2)
            return out.reshape(b, h, n, d)

        def attn_layer(x, Wqkv, qs, ksc, Wo):
            b, n, _ = x.shape
            qkv = x @ Wqkv
            q, k, v = jnp.split(qkv, 3, -1)
            sh = lambda t: t.reshape(b, n, HEADS, DIM_HEAD).transpose(0, 2, 1, 3)
            q, k, v = (sh(q), sh(k), sh(v))
            q = l2norm(q) * qs
            k = l2norm(k) * ksc
            freqs, scale = rotary_tables(n)
            cos, sin = (jnp.cos(freqs), jnp.sin(freqs))
            q = q * cos * scale + rotate_half(q) * sin * scale
            inv = 1.0 / scale
            k = k * cos * inv + rotate_half(k) * sin * inv
            out = local_attention(q, k, v)
            out = out.transpose(0, 2, 1, 3).reshape(b, n, INNER)
            return out @ Wo

        def ffn_layer(x, g, bln, W1, b1, W2, b2):
            mu = x.mean(-1, keepdims=True)
            var = ((x - mu) ** 2).mean(-1, keepdims=True)
            xn = (x - mu) / jnp.sqrt(var + 1e-05) * g + bln
            hg = xn @ W1 + b1
            a, gate = jnp.split(hg, 2, -1)
            return a * jax.nn.gelu(gate, approximate=False) @ W2 + b2
        for i in range(DEPTH):
            x = attn_layer(shift_tokens(x), Wqkv[i], q_scale[i], k_scale[i], Wo[i]) + x
            x = ffn_layer(shift_tokens(x), ln_g[i], ln_b[i], W1[i], b1[i], W2[i], b2[i]) + x
        return x
    x = L0_attn_x
    x = _layernorm(x + _L0_attn_ref(x, L0_attn_P_q, L0_attn_P_k, L0_attn_P_v, L0_attn_P_o), axis=-1)
    x = _layernorm(x + _L0_ffn_ref(x, L0_ffn_Wqkv, L0_ffn_q_scale, L0_ffn_k_scale, L0_ffn_Wo, L0_ffn_ln_g, L0_ffn_ln_b, L0_ffn_W1, L0_ffn_b1, L0_ffn_W2, L0_ffn_b2), axis=-1)
    return x

_drawn_inputs = setup_inputs


def setup_inputs(seed=0):
    import zlib

    import numpy as np

    out = dict(_drawn_inputs(seed))
    spreads = {'L0_ffn_q_scale': (1.0, 0.6),
     'L0_ffn_k_scale': (1.0, 0.6),
     'L0_ffn_ln_g': (1.0, 0.6),
     'L0_ffn_ln_b': (0.0, 0.8),
     'L0_ffn_b1': (0.0, 0.8),
     'L0_ffn_b2': (0.0, 0.1)}
    factors = {'L0_attn_P_q': 6.172,
     'L0_attn_P_k': 6.139,
     'L0_attn_P_v': 4.443,
     'L0_attn_P_o': 4.449,
     'L0_ffn_W1': 3.672,
     'L0_ffn_W2': 3.608}
    for name, (base, spread) in spreads.items():
        noise = np.random.default_rng([zlib.crc32(name.encode()), seed]).standard_normal(out[name].shape)
        drawn = base * np.exp(spread * noise) if base else spread * noise
        out[name] = jnp.asarray(drawn.astype(out[name].dtype))
    for name, factor in factors.items():
        out[name] = (out[name] * factor).astype(out[name].dtype)
    return out
```

```python
from contextlib import ExitStack

import numpy as np
import concourse.bass as bass
from concourse import mybir

F32 = mybir.dt.float32
F32R = mybir.dt.float32r
BF16 = mybir.dt.bfloat16
ALU = mybir.AluOpType
ACT = mybir.ActivationFunctionType
AX = mybir.AxisListType

NB = 8
T = 512
D = 128
P = 128
MT = T // P
H = 16
DH = 64
DEPTH = 6
WIN = 32
G = 4
HG = H // G
CQ = HG * DH
WP = T // (2 * WIN)
KW = 3 * WIN
XC = WIN + T
DI = int(D * 4 * 2 / 3)
FCH = [(o, min(P, DI - o)) for o in range(0, DI, P)]
NF = len(FCH)
STEPS = H
NEG = -1e30
LN_EPS = 1e-5


def ge(engine, sem, count):
    if isinstance(count, int) and count <= 0:
        return
    engine.wait_ge(sem, count)


class At:

    def __init__(self, b, c):
        self.k = b * STEPS + c
        self.pos = c % STEPS
        self.batch = b + c // STEPS
        self.group = b * G + c // HG
        self.g, self.m = self.pos // MT, self.pos % MT
        self.par, self.gpar = self.pos % 2, self.g % 2


def at(b, j, lag):
    c = j - lag
    if isinstance(b, int) and not 0 <= b * STEPS + c < NB * STEPS:
        return None
    return At(b, c)


def every_step(engine, step, drain):
    for b in range(2):
        for j in range(STEPS):
            step(b, j)
    with engine.Fori(2, NB) as b:
        for j in range(STEPS):
            step(b, j)
    for j in range(drain):
        step(NB, j)


def tokens(X, batch):
    return X[:, batch * T:(batch + 1) * T] if isinstance(batch, int) else X[:, bass.ts(batch, T)]


def first_attention(nc, dram, X, ident, banks):
    with ExitStack() as ctx:
        sb = lambda name, shape, dt=F32: ctx.enter_context(nc.sbuf_tensor("f_" + name, shape, dt))
        sem = lambda name: ctx.enter_context(nc.semaphore("f_" + name))
        pq_sb, pk_sb = sb("pq_sb", [DH, H * D]), sb("pk_sb", [DH, H * D])
        pv_sb = sb("pv_sb", [P, H * DH])
        po_sb = sb("po_sb", [P, 8, D])
        mh, ml = sb("mh", [P, H, D], F32R), sb("ml", [P, H, D], F32R)
        pvh, pvl = sb("pvh", [P, H * DH], F32R), sb("pvl", [P, H * DH], F32R)
        x_cur = sb("x_cur", [P, T])
        xh, xl = sb("xh", [P, T], F32R), sb("xl", [P, T], F32R)
        yh, yl = sb("yh", [P, 2, T], F32R), sb("yl", [P, 2, T], F32R)
        E = sb("E", [P, 2, MT, T])
        diag_only = sb("diag_only", [P, MT, P])
        ident_b, mask_b, mask_f = sb("ident_b", [P, P], BF16), sb("mask_b", [P, P], BF16), sb("mask_f", [P, P])
        negmax, esum = sb("negmax", [P, 2, MT]), sb("esum", [P, 4, MT])
        ediag, erec = sb("ediag", [P, 2, MT]), sb("erec", [P, 2, MT])
        prob, prob_all = sb("prob", [P, MT, H]), sb("prob_all", [P, MT, H])
        V = sb("V", [P, MT, H * DH])
        O = sb("O", [P, 2, T])
        OT = sb("OT", [P, 2, MT, P])
        xn = sb("xn", [P, T])
        st, ag = sb("st", [P, MT, 6]), sb("ag", [P, MT, 2])
        ve, rstd, mhalf = sb("ve", [P, MT]), sb("rstd", [P, MT]), sb("mhalf", [P, MT])
        p_y, p_s, p_v, p_t, p_z = banks[0], banks[1:5], banks[5], banks[6], banks[7]

        loaded, m_made, w_hi, w_lo, masks_made = (sem(n) for n in ("loaded", "m_made", "w_hi", "w_lo", "masks_made"))
        xc_ready, xt_ready, xh_ready, xl_ready = (sem(n) for n in ("xc_ready", "xt_ready", "xh_ready", "xl_ready"))
        y_ready, yh_ready, yl_ready = (sem(n) for n in ("y_ready", "yh_ready", "yl_ready"))
        logits_ready, max_ready, exp_ready = (sem(n) for n in ("logits_ready", "max_ready", "exp_ready"))
        diag_ready, rec_ready, prob_ready, all_ready = (sem(n) for n in ("diag_ready", "rec_ready", "prob_ready", "all_ready"))
        v_ready, v_out, o_ready, ot_ready, ot_out, z_ready = (sem(n) for n in ("v_ready", "v_out", "o_ready", "ot_ready", "ot_out", "z_ready"))
        sum_ready, stats_ready, aggr_ready, var_ready, rstd_ready, x_out = (sem(n) for n in ("sum_ready", "stats_ready", "aggr_ready", "var_ready", "rstd_ready", "x_out"))
        half_set = sem("half_set")

        with nc.Block() as block:

            @block.sync
            def _(sp):
                for dst, src in ((X[:, :].rearrange("p (n d) -> p n d", d=D), dram["x"]), (pq_sb[:, :], dram["pqt"]),
                                 (pk_sb[:, :], dram["pkt"]), (pv_sb[:, :], dram["pv"]),
                                 (po_sb[:, :, :], dram["po"]), (mask_f[:, :], dram["causal"])):
                    sp.dma_start(dst, src).then_inc(loaded, 16)
                sp.wait_ge(loaded, 96)
                sp.dma_start(x_cur[:, :], X[:, 0:T]).then_inc(xc_ready, 16)
                with sp.Fori(1, NB) as b:
                    sp.wait_ge(xt_ready, b)
                    sp.dma_start(x_cur[:, :], tokens(X, b)).then_inc(xc_ready, 16)

            @block.tensor
            def _(pe):
                pe.wait_ge(loaded, 96)
                for q in range(4):
                    for h in range(4 * q, 4 * q + 4):
                        ins = pe.matmul(p_s[q][:, h % 4 * P:(h % 4 + 1) * P], pq_sb[:, h * D:(h + 1) * D],
                                        pk_sb[:, h * D:(h + 1) * D], start=True, stop=True)
                    ins.then_inc(m_made, 1)
                pe.wait_ge(w_lo, 5)
                pe.wait_ge(masks_made, 2)

                def step(b, j):
                    a = at(b, j, 0)
                    if a and j == 0:
                        pe.wait_ge(xc_ready, b * 16 + 16)
                        ge(pe, ot_out, b * 8 - 8)
                        for i in range(MT):
                            ins = pe.transpose(p_t[:, i * P:(i + 1) * P], x_cur[:, i * P:(i + 1) * P], ident[:, :])
                        ins.then_inc(xt_ready, 1)
                    def logits():
                        s = at(b, j, 1)
                        if s:
                            pe.wait_ge(yl_ready, s.k + 1)
                            for i in range(MT):
                                ge(pe, exp_ready, (s.k - 1) * MT + i + 1)
                                w, q = max(2 * P, (i + 1) * P), slice(i * P, (i + 1) * P)
                                pe.matmul(p_s[i][:, 0:w], yh[:, s.par, q], xh[:, 0:w], start=True, stop=False)
                                pe.matmul(p_s[i][:, 0:w], yl[:, s.par, q], xh[:, 0:w], start=False, stop=False)
                                pe.matmul(p_s[i][:, 0:w], yh[:, s.par, q], xl[:, 0:w], start=False, stop=True)
                                pe.matmul(p_s[i][:, q], ident_b[:, :], mask_b[:, :], start=False, stop=True,
                                          skip_group_check=True).then_inc(logits_ready, 1)

                    def projected():
                        if a:
                            if j == 0:
                                pe.wait_ge(xl_ready, b + 1)
                            ge(pe, yl_ready, a.k)
                            pe.matmul(p_y[:, :], mh[:, a.pos, :], xh[:, :], start=True, stop=False)
                            pe.matmul(p_y[:, :], ml[:, a.pos, :], xh[:, :], start=False, stop=False)
                            pe.matmul(p_y[:, :], mh[:, a.pos, :], xl[:, :], start=False, stop=True).then_inc(y_ready, 1)

                    for stage in (logits, projected) if j == 0 else (projected, logits):
                        stage()
                    if a and j >= 8:
                        i, half = divmod(j - 8, 2)
                        ge(pe, v_out, b * 8 + j - 8)
                        q, c = slice(i * P, (i + 1) * P), slice(half * T, half * T + T)
                        pe.matmul(p_v[:, :], xh[:, q], pvh[:, c], start=True, stop=False)
                        pe.matmul(p_v[:, :], xl[:, q], pvh[:, c], start=False, stop=False)
                        pe.matmul(p_v[:, :], xh[:, q], pvl[:, c], start=False, stop=True).then_inc(v_ready, 1)
                    o = at(b, j, STEPS)
                    if o and 5 <= j < 13:
                        i, half = divmod(j - 5, 2)
                        pe.wait_ge(ot_out, o.batch * 8 + j - 4)
                        if j == 5:
                            ge(pe, sum_ready, o.batch)
                        for c in range(4):
                            ins = pe.matmul(p_z[:, i * P:(i + 1) * P], OT[:, half, c, :], po_sb[:, 4 * half + c, :],
                                            start=(half + c == 0), stop=(half == 1 and c == 3))
                        ins.then_inc(z_ready, 1)
                    if o and 4 <= j < 12:
                        pe.wait_ge(o_ready, o.batch * 8 + j - 3)
                        ge(pe, ot_out, o.batch * 8 + j - 4)
                        if j == 4:
                            pe.wait_ge(xl_ready, NB if isinstance(b, int) and b == NB else o.batch + 2)
                        for c in range(4):
                            ins = pe.transpose(p_t[:, c * P:(c + 1) * P], O[:, j % 2, c * P:(c + 1) * P], ident[:, :])
                        ins.then_inc(ot_ready, 1)

                every_step(pe, step, STEPS)

            @block.scalar
            def _(act):
                act.wait_ge(loaded, 96)
                for q in range(4):
                    act.wait_ge(m_made, q + 1)
                    act.activation(mh[:, 4 * q:4 * q + 4, :], p_s[q][:, :].rearrange("p (a b) -> p a b", a=4),
                                   ACT.Copy, scale=8.0).then_inc(w_hi, 1)
                act.activation(pvh[:, :], pv_sb[:, :], ACT.Copy).then_inc(w_hi, 1)

                def step(b, j):
                    a = at(b, j, 0)
                    if a and j == 0:
                        act.wait_ge(xt_ready, b + 1)
                        ge(act, logits_ready, b * STEPS * MT)
                        ge(act, v_ready, b * 8)
                        act.activation(xh[:, :], p_t[:, :], ACT.Copy).then_inc(xh_ready, 1)
                    if a:
                        act.wait_ge(y_ready, a.k + 1)
                        ge(act, logits_ready, (a.k - 1) * MT)
                        act.activation(yh[:, a.par, :], p_y[:, :], ACT.Copy).then_inc(yh_ready, 1)
                    s = at(b, j, 1)
                    if s:
                        for i in range(MT):
                            act.wait_ge(max_ready, s.k * MT + i + 1)
                            ge(act, diag_ready, (s.k - 2) * MT + i + 1)
                            if i == 0:
                                ge(act, rec_ready, s.k - 3)
                            w = (i + 1) * P
                            act.activation(E[:, s.par, i, 0:w], p_s[i][:, 0:w], ACT.Exp, bias=negmax[:, s.par, i:i + 1],
                                           accum_out=esum[:, s.pos % 4, i:i + 1]).then_inc(exp_ready, 1)
                    if a and j >= 8:
                        i, half = divmod(j - 8, 2)
                        act.wait_ge(v_ready, b * 8 + j - 7)
                        ge(act, o_ready, (b - 1) * 8 + j - 7)
                        act.activation(V[:, i, half * T:half * T + T], p_v[:, :], ACT.Copy).then_inc(v_out, 1)
                    o = at(b, j, STEPS)
                    if o and 4 <= j < 12:
                        act.wait_ge(ot_ready, o.batch * 8 + j - 3)
                        ge(act, z_ready, o.batch * 8 + j - 5)
                        act.activation(OT[:, j % 2, :, :], p_t[:, :].rearrange("p (c t) -> p c t", c=4),
                                       ACT.Copy).then_inc(ot_out, 1)

                every_step(act, step, STEPS)

            @block.gpsimd
            def _(pool):
                pool.memset(mhalf[:, :], -0.5).then_inc(half_set, 1)
                pool.wait_ge(half_set, 1)

                def step(b, j):
                    o = at(b, j, STEPS)
                    if o and 3 <= j < 11:
                        i, half = divmod(j - 3, 2)
                        pool.wait_ge(v_out, o.batch * 8 + j - 2)
                        pool.wait_ge(all_ready, o.batch + 1)
                        ge(pool, ot_ready, o.batch * 8 + j - 4)
                        heads = prob_all[:, i, 8 * half:8 * half + 8].unsqueeze(2).to_broadcast([P, 8, DH])
                        pool.tensor_tensor(O[:, half, :].rearrange("p (h f) -> p h f", f=DH),
                                           V[:, i, half * T:half * T + T].rearrange("p (h f) -> p h f", f=DH),
                                           heads, ALU.mult).then_inc(o_ready, 1)
                    if o and j == 13:
                        pool.wait_ge(var_ready, o.batch + 1)
                        pool.tensor_tensor(rstd[:, :], ve[:, :], mhalf[:, :], ALU.pow).then_inc(rstd_ready, 1)

                every_step(pool, step, STEPS)

            @block.vector
            def _(dve):
                dve.wait_ge(loaded, 96)
                dve.tensor_copy(mask_b[:, :], mask_f[:, :]).then_inc(masks_made, 1)
                dve.tensor_copy(ident_b[:, :], ident[:, :]).then_inc(masks_made, 1)
                for q in range(4):
                    dve.wait_ge(w_hi, q + 1)
                    dve.scalar_tensor_tensor(ml[:, 4 * q:4 * q + 4, :].rearrange("p a b -> p (a b)"), p_s[q][:, :], 8.0,
                                             mh[:, 4 * q:4 * q + 4, :].rearrange("p a b -> p (a b)").bitcast(F32),
                                             ALU.mult, ALU.subtract).then_inc(w_lo, 1)
                dve.wait_ge(w_hi, 5)
                dve.tensor_tensor(pvl[:, :], pv_sb[:, :], pvh[:, :].bitcast(F32), ALU.subtract).then_inc(w_lo, 1)

                def step(b, j):
                    a = at(b, j, 0)
                    if a and j == 0:
                        dve.wait_ge(xh_ready, b + 1)
                        dve.tensor_tensor(xl[:, :], p_t[:, :], xh[:, :].bitcast(F32), ALU.subtract).then_inc(xl_ready, 1)
                    if a:
                        dve.wait_ge(yh_ready, a.k + 1)
                        dve.tensor_tensor(yl[:, a.par, :], p_y[:, :], yh[:, a.par, :].bitcast(F32),
                                          ALU.subtract).then_inc(yl_ready, 1)
                    g = at(b, j, 3)
                    if g:
                        for i in range(MT):
                            dve.wait_ge(exp_ready, g.k * MT + i + 1)
                            if i == 0:
                                ge(dve, prob_ready, g.k - 1)
                            ge(dve, diag_ready, (g.k - 1) * MT + i + 1)
                            dve.scalar_tensor_tensor(diag_only[:, i, :], E[:, g.par, i, i * P:(i + 1) * P], 1.0, ident[:, :], ALU.mult,
                                                     ALU.mult, accum_out=ediag[:, g.par, i:i + 1]).then_inc(diag_ready, 1)
                    s = at(b, j, 1)
                    if s:
                        for i in range(MT):
                            dve.wait_ge(logits_ready, s.k * MT + i + 1)
                            if i == 0:
                                ge(dve, exp_ready, (s.k - 1) * MT)
                            dve.tensor_reduce(negmax[:, s.par, i:i + 1], p_s[i][:, 0:(i + 1) * P], AX.X, ALU.max,
                                              negate=True).then_inc(max_ready, 1)
                    r = at(b, j, 4)
                    if r:
                        dve.reciprocal(erec[:, r.par, :], esum[:, r.pos % 4, :]).then_inc(rec_ready, 1)
                        dve.wait_ge(rec_ready, r.k + 1)
                        dve.wait_ge(diag_ready, (r.k + 1) * MT)
                        dve.tensor_tensor(prob[:, :, r.pos], ediag[:, r.par, :], erec[:, r.par, :],
                                          ALU.mult).then_inc(prob_ready, 1)
                        if r.pos == H - 1:
                            dve.wait_ge(prob_ready, r.k + 1)
                            ge(dve, o_ready, r.batch * 8)
                            dve.tensor_copy(prob_all[:, :, :], prob[:, :, :]).then_inc(all_ready, 1)
                    o = at(b, j, STEPS)
                    if o and j == 13:
                        dve.wait_ge(z_ready, (o.batch + 1) * 8)
                        ge(dve, x_out, o.batch)
                        dve.tensor_tensor(xn[:, :], tokens(X, o.batch), p_z[:, :], ALU.add).then_inc(sum_ready, 1)
                        dve.wait_ge(sum_ready, o.batch + 1)
                        statistics(dve, xn, st, ag, ve, stats_ready, aggr_ready, var_ready, o.batch)
                    if o and j == 14:
                        normalise(dve, xn, ag, rstd, rstd_ready, tokens(X, o.batch), x_out, o.batch)

                every_step(dve, step, STEPS)


def statistics(dve, x, st, ag, ve, stats_ready, aggr_ready, var_ready, n):
    for i in range(MT):
        ins = dve.bn_stats(st[:, i, :], x[:, i * D:(i + 1) * D])
    ins.then_inc(stats_ready, 1)
    dve.wait_ge(stats_ready, n + 1)
    dve.memset(ve[:, :], 0.0)
    for i in range(MT):
        ins = dve.bn_aggr(ag[:, i, :], st[:, i, :])
    ins.then_inc(aggr_ready, 1)
    dve.wait_ge(aggr_ready, n + 1)
    dve.tensor_scalar(ve[:, :], ag[:, :, 1], LN_EPS, None, ALU.add).then_inc(var_ready, 1)


def normalise(dve, x, ag, rstd, rstd_ready, out, done, n):
    dve.wait_ge(rstd_ready, n + 1)
    for i in range(MT):
        ins = dve.tensor_scalar(out[:, i * D:(i + 1) * D], x[:, i * D:(i + 1) * D], ag[:, i, 0:1], rstd[:, i:i + 1],
                                ALU.subtract, ALU.mult)
    ins.then_inc(done, 1)


class Weights:

    def __init__(self, nc, ctx):
        sb = lambda name, shape: ctx.enter_context(nc.sbuf_tensor(name, shape, F32))
        self.qkv = sb("w_qkv", [P, G, 3 * CQ])
        self.scales = sb("w_scales", [P, 2, DH])
        self.out = sb("w_out", [P, 8, D])
        self.w1 = sb("w_w1", [P, 2 * DI])
        self.w2 = sb("w_w2", [P, NF, D])
        self.cols = sb("w_cols", [P, 2 + 2 * NF])
        self.b2 = sb("w_b2", [P, D])

    def attention_loads(self, dram, layer):
        return ((self.qkv[:, :, :], dram["qkv"][layer]), (self.out[:, :, :], dram["wo"][layer]),
                (self.scales[:, :, :], dram["scales"][layer].partition_broadcast(P)))

    def feed_forward_loads(self, dram, layer):
        return ((self.w1[:, :], dram["w1"][layer]), (self.w2[:, :, :], dram["w2"][layer]),
                (self.cols[:, :], dram["cols"][layer]), (self.b2[:, :], dram["b2"][layer].partition_broadcast(P)))


def windowed_attention(nc, dram, X, ident, banks, w, layer, S):
    with ExitStack() as ctx:
        sb = lambda name, shape, dt=F32: ctx.enter_context(nc.sbuf_tensor("a_" + name, shape, dt))
        wh, wl = sb("wh", [P, G, 3 * CQ], F32R), sb("wl", [P, G, 3 * CQ], F32R)
        tabs_c, tabs_s = sb("tabs_c", [P, MT, 2, DH]), sb("tabs_s", [P, MT, 2, DH])
        rot_c, rot_s = sb("rot_c", [P, MT, 2, DH]), sb("rot_s", [P, MT, 2, DH])
        masks_f, masks = sb("masks_f", [P, 2, KW]), sb("masks", [P, 2, KW], BF16)
        ident_b = sb("ident_b", [P, P], BF16)
        minus_half = sb("minus_half", [P, 2 * HG])
        x_cur = sb("x_cur", [P, T])
        xh, xl = sb("xh", [P, XC], F32R), sb("xl", [P, XC], F32R)
        sq = sb("sq", [P, 2, 2 * CQ])
        ssq, ssqc, rn = sb("ssq", [P, 2, 2 * HG]), sb("ssqc", [P, 2, 2 * HG]), sb("rn", [P, 2, 2 * HG])
        qn, u, v, r = (sb(n, [P, 2, 2 * CQ]) for n in ("qn", "u", "v", "r"))
        QT = sb("QT", [P, 2, 2, WP, P])
        KT = sb("KT", [P, 2, 2, XC])
        V = sb("V", [KW, G, WP, CQ])
        E, PN = sb("E", [P, 2, 4, KW]), sb("PN", [P, 2, 4, KW])
        negmax, esum, erec = sb("negmax", [P, 2, 4]), sb("esum", [P, 2, 4]), sb("erec", [P, 2, 4])
        PT = sb("PT", [KW, 2, 4, P])
        OT = sb("OT", [P, 2, 2, T])
        p_qk, p_v, p_t, p_s, p_p, p_o, p_y = banks[0:2], banks[2], banks[3], banks[4], banks[5], banks[6], banks[7]

        with nc.Block() as block:

            @block.sync
            def _(sp):
                for dst, src in ((tabs_c[:, :, :, :], dram["rot_cos"]), (tabs_s[:, :, :, :], dram["rot_sin"]),
                                 (masks_f[:, :, :], dram["windows"])):
                    sp.dma_start(dst, src).then_inc(S["consts"], 16)
                sp.dma_start(x_cur[:, :], X[:, 0:T]).then_inc(S["xc"], 16)
                for dst, src in w.feed_forward_loads(dram, layer):
                    sp.dma_start(dst, src).then_inc(S["weights"], 16)
                with sp.Fori(1, NB) as b:
                    sp.wait_ge(S["xt"], b)
                    sp.dma_start(x_cur[:, :], tokens(X, b)).then_inc(S["xc"], 16)
                sp.wait_ge(S["weights"], 64)

            @block.tensor
            def _(pe):
                pe.wait_ge(S["const_made"], 3)
                pe.wait_ge(S["w_lo"], G)

                def step(b, j):
                    a = at(b, j, 0)
                    if a and j == 0:
                        pe.wait_ge(S["xc"], b * 16 + 16)
                        ge(pe, S["k_out"], a.k - 2)
                        ge(pe, S["q_out"], a.k - 2)
                        for i in range(MT):
                            ins = pe.transpose(p_t[:, i * P:(i + 1) * P], x_cur[:, i * P:(i + 1) * P], ident[:, :])
                        ins.then_inc(S["xt"], 1)
                    o = at(b, j, 8)
                    if o:
                        pe.wait_ge(S["pt_out"], o.k + 1)
                        pe.wait_ge(S["v_out"], o.k - o.m + 4)
                        ge(pe, S["o_out"], o.k)
                        hp, half = divmod(o.m, 2)
                        for n in range(4):
                            ins = pe.matmul(p_o[:, n * P:(n + 1) * P], V[:, o.g, 4 * half + n, hp * P:(hp + 1) * P],
                                            PT[:, o.par, n, :], start=True, stop=True)
                        ins.then_inc(S["o"], 1)
                    y = at(b, j, 9)
                    if y and y.m == 3:
                        pe.wait_ge(S["o_out"], y.k + 1)
                        if y.g == 0:
                            ge(pe, S["x_out"], y.batch)
                        for i in range(MT):
                            for hp in range(2):
                                ins = pe.matmul(p_y[:, i * P:(i + 1) * P], OT[:, y.gpar, hp, i * P:(i + 1) * P],
                                                w.out[:, 2 * y.g + hp, :], start=(y.g + i + hp == 0),
                                                stop=(y.g == G - 1 and hp == 1), skip_group_check=True)
                        ins.then_inc(S["y"], 1)
                    t = at(b, j, 7)
                    if t:
                        pe.wait_ge(S["pn"], t.k + 1)
                        ge(pe, S["pt_out"], t.k)
                        for n in range(4):
                            ins = pe.transpose(p_p[0:KW, n * P:(n + 1) * P], PN[:, t.par, n, :], ident[:, :])
                        ins.then_inc(S["pt"], 1)
                    s = at(b, j, 6)
                    if s:
                        pe.wait_ge(S["k_out"], s.k - s.m + 4)
                        pe.wait_ge(S["q_out"], s.k - s.m + 4)
                        ge(pe, S["exp"], s.k)
                        hp, half = divmod(s.m, 2)
                        for n in range(4):
                            first = 64 * (4 * half + n)
                            cols = slice(n * KW, (n + 1) * KW)
                            pe.matmul(p_s[:, cols], ident_b[:, :], masks[:, int(first > 0), :], start=True, stop=False)
                            ins = pe.matmul(p_s[:, cols], QT[:, s.gpar, hp, 4 * half + n, :],
                                            KT[:, s.gpar, hp, first:first + KW], start=False, stop=True)
                        ins.then_inc(S["logits"], 1)
                    t = at(b, j, 2)
                    if t:
                        pe.wait_ge(S["r"], t.k + 1)
                        ge(pe, S["k_out"], t.k)
                        ge(pe, S["q_out"], t.k)
                        if t.pos == STEPS - 2:
                            pe.wait_ge(S["xl"], NB if isinstance(b, int) and b == NB else t.batch + 2)
                        for c in range(4):
                            ins = pe.transpose(p_t[:, c * P:(c + 1) * P], r[:, t.par, c * P:(c + 1) * P], ident[:, :])
                        ins.then_inc(S["qkt"], 1)
                    if a:
                        if j == 0:
                            pe.wait_ge(S["xl"], b + 1)
                        ge(pe, S["sq"], a.k - 1)
                        ge(pe, S["qn"], a.k - 1)
                        m, g = slice(WIN + a.m * P, WIN + (a.m + 1) * P), a.g
                        pe.matmul(p_qk[a.par][:, :], xh[:, m], wh[:, g, 0:2 * CQ], start=True, stop=False)
                        pe.matmul(p_qk[a.par][:, :], xl[:, m], wh[:, g, 0:2 * CQ], start=False, stop=False)
                        pe.matmul(p_qk[a.par][:, :], xh[:, m], wl[:, g, 0:2 * CQ], start=False, stop=True).then_inc(S["qk"], 1)
                        ge(pe, S["v_out"], a.k)
                        for n in range(2):
                            m = slice(64 * (2 * a.m + n), 64 * (2 * a.m + n) + KW)
                            to, c = p_v[0:KW, n * CQ:(n + 1) * CQ], slice(2 * CQ, 3 * CQ)
                            pe.matmul(to, xh[:, m], wh[:, g, c], start=True, stop=False)
                            pe.matmul(to, xl[:, m], wh[:, g, c], start=False, stop=False)
                            ins = pe.matmul(to, xh[:, m], wl[:, g, c], start=False, stop=True)
                        ins.then_inc(S["v"], 1)

                every_step(pe, step, 10)

            @block.scalar
            def _(act):
                for g in range(G):
                    act.activation(wh[:, g, :], w.qkv[:, g, :], ACT.Copy).then_inc(S["w_hi"], 1)

                def step(b, j):
                    a = at(b, j, 0)
                    if a and j == 0:
                        act.wait_ge(S["xt"], b + 1)
                        act.wait_ge(S["pads"], 4)
                        ge(act, S["v"], a.k)
                        act.activation(xh[0:64, WIN:XC], p_t[0:64, :], ACT.Copy)
                        act.activation(xh[64:P, WIN + 1:XC], p_t[64:P, 0:T - 1], ACT.Copy).then_inc(S["xh"], 1)
                    o = at(b, j, 8)
                    if o:
                        act.wait_ge(S["o"], o.k + 1)
                        ge(act, S["y"], o.group - 1)
                        hp, half = divmod(o.m, 2)
                        for h in range(2):
                            q = slice(64 * h, 64 * h + 64)
                            ins = act.activation(
                                OT[q, o.gpar, hp, 4 * 64 * half:4 * 64 * (half + 1)].rearrange("p (n t) -> p n t", n=4),
                                p_o[q, :].rearrange("p (n h t) -> p n h t", n=4, h=2)[:, :, h, :], ACT.Copy)
                        ins.then_inc(S["o_out"], 1)
                    t = at(b, j, 7)
                    if t:
                        act.wait_ge(S["pt"], t.k + 1)
                        ge(act, S["o"], t.k - 1)
                        act.activation(PT[:, t.par, :, :], p_p[0:KW, :].rearrange("p (n q) -> p n q", n=4),
                                       ACT.Copy).then_inc(S["pt_out"], 1)
                    s = at(b, j, 6)
                    if s:
                        act.wait_ge(S["max"], s.k + 1)
                        ge(act, S["pn"], s.k - 1)
                        for n in range(4):
                            ins = act.activation(E[:, s.par, n, :], p_s[:, n * KW:(n + 1) * KW], ACT.Exp,
                                                 bias=negmax[:, s.par, n:n + 1], accum_out=esum[:, s.par, n:n + 1])
                        ins.then_inc(S["exp"], 1)
                    t = at(b, j, 2)
                    if t:
                        act.wait_ge(S["qkt"], t.k + 1)
                        ge(act, S["logits"], t.k - t.m - 4)
                        c = WIN + t.m * P
                        act.activation(KT[:, t.gpar, :, c:c + P], p_t[:, 2 * P:].rearrange("p (h t) -> p h t", h=2),
                                       ACT.Copy).then_inc(S["k_out"], 1)
                    if a:
                        act.wait_ge(S["qk"], a.k + 1)
                        ge(act, S["red"], a.k - 1)
                        act.activation(sq[:, a.par, :], p_qk[a.par][:, :], ACT.Square).then_inc(S["sq"], 1)
                        act.wait_ge(S["v"], a.k + 1)
                        ge(act, S["o"], a.k - a.m - 12)
                        act.activation(V[:, a.g, 2 * a.m:2 * a.m + 2, :],
                                       p_v[0:KW, :].rearrange("p (n c) -> p n c", n=2), ACT.Copy).then_inc(S["v_out"], 1)

                every_step(act, step, 10)

            @block.gpsimd
            def _(pool):
                pool.memset(minus_half[:, :], -0.5).then_inc(S["const_made"], 1)
                pool.memset(QT[:, :, :, :, :], 0.0).then_inc(S["pads"], 1)
                pool.memset(KT[:, :, :, 0:WIN], 0.0).then_inc(S["pads"], 1)
                pool.wait_ge(S["const_made"], 1)

                def step(b, j):
                    a = at(b, j, 1)
                    if a:
                        pool.wait_ge(S["qn"], a.k + 1)
                        ge(pool, S["r"], a.k - 1)
                        if isinstance(b, int) and a.k == 0:
                            pool.wait_ge(S["rot"], 1 + MT)
                        view = lambda x: x[:, a.par, :].rearrange("p (s h f) -> p s h f", s=2, h=HG)
                        tab = rot_c[:, a.m, :, :].unsqueeze(2).to_broadcast([P, 2, HG, DH])
                        pool.tensor_tensor(view(u), view(qn), tab, ALU.mult).then_inc(S["u"], 1)
                    s = at(b, j, 6)
                    if s:
                        pool.wait_ge(S["rec"], s.k + 1)
                        ge(pool, S["pt"], s.k - 1)
                        pool.tensor_tensor(PN[:, s.par, :, :], E[:, s.par, :, :],
                                           erec[:, s.par, :].unsqueeze(2).to_broadcast([P, 4, KW]),
                                           ALU.mult).then_inc(S["pn"], 1)
                    a = at(b, j, 0)
                    if a:
                        pool.wait_ge(S["red"], a.k + 1)
                        ge(pool, S["qn"], a.k - 1)
                        pool.tensor_tensor(rn[:, a.par, :], ssqc[:, a.par, :], minus_half[:, :], ALU.pow).then_inc(S["rn"], 1)

                every_step(pool, step, 10)

            @block.vector
            def _(dve):
                dve.memset(xh[:, 0:WIN + 2].bitcast(F32), 0.0).then_inc(S["pads"], 1)
                dve.memset(xl[:, 0:WIN + 2].bitcast(F32), 0.0).then_inc(S["pads"], 1)
                dve.wait_ge(S["consts"], 48)
                dve.tensor_copy(masks[:, :, :], masks_f[:, :, :]).then_inc(S["const_made"], 1)
                dve.tensor_copy(ident_b[:, :], ident[:, :]).then_inc(S["const_made"], 1)
                for g in range(G):
                    dve.wait_ge(S["w_hi"], g + 1)
                    dve.tensor_tensor(wl[:, g, :], w.qkv[:, g, :], wh[:, g, :].bitcast(F32), ALU.subtract).then_inc(S["w_lo"], 1)
                dve.tensor_tensor(rot_c[:, :, :, :].rearrange("p m s f -> p m (s f)"),
                                  tabs_c[:, :, :, :].rearrange("p m s f -> p m (s f)"),
                                  w.scales[:, :, :].rearrange("p s f -> p (s f)").unsqueeze(1).to_broadcast([P, MT, 2 * DH]),
                                  ALU.mult).then_inc(S["rot"], 1)
                swap = lambda x: x.rearrange("p s (h f) -> p s h f", h=2)
                for m in range(MT):
                    dve.tensor_tensor(swap(rot_s[:, m, :, :]), swap(tabs_s[:, m, :, :]), swap(w.scales[:, :, :])[:, :, ::-1, :],
                                      ALU.mult).then_inc(S["rot"], 1)
                dve.wait_ge(S["rot"], 1 + MT)
                dve.wait_ge(S["pads"], 4)

                def step(b, j):
                    a = at(b, j, 0)
                    if a and j == 0:
                        dve.wait_ge(S["xh"], b + 1)
                        dve.tensor_tensor(xl[0:64, WIN:XC], p_t[0:64, :], xh[0:64, WIN:XC].bitcast(F32), ALU.subtract)
                        dve.tensor_tensor(xl[64:P, WIN + 1:XC], p_t[64:P, 0:T - 1], xh[64:P, WIN + 1:XC].bitcast(F32),
                                          ALU.subtract).then_inc(S["xl"], 1)
                    s = at(b, j, 6)
                    if s:
                        dve.wait_ge(S["logits"], s.k + 1)
                        ge(dve, S["exp"], s.k - 1)
                        dve.tensor_reduce(negmax[:, s.par, :], p_s[:, 0:4 * KW].rearrange("p (n k) -> p n k", n=4), AX.X,
                                          ALU.max, negate=True).then_inc(S["max"], 1)
                    c = at(b, j, 1)
                    if c:
                        dve.wait_ge(S["rn"], c.k + 1)
                        ge(dve, S["u"], c.k - 1)
                        ge(dve, S["v_rot"], c.k - 1)
                        heads = lambda x: x.rearrange("p (h f) -> p h f", f=DH)
                        dve.tensor_tensor(heads(qn[:, c.par, :]), heads(p_qk[c.par][:, :]),
                                          rn[:, c.par, :].unsqueeze(2).to_broadcast([P, 2 * HG, DH]),
                                          ALU.mult).then_inc(S["qn"], 1)
                        dve.wait_ge(S["qn"], c.k + 1)
                        ge(dve, S["r"], c.k - 1)
                        halves = lambda x: x.rearrange("p (s h t f) -> p s h t f", s=2, h=HG, t=2)
                        tab = rot_s[:, c.m, :, :].rearrange("p s (t f) -> p s t f", t=2).unsqueeze(2).to_broadcast([P, 2, HG, 2, DH // 2])
                        dve.tensor_tensor(halves(v[:, c.par, :]), halves(qn[:, c.par, :])[:, :, :, ::-1, :], tab,
                                          ALU.mult).then_inc(S["v_rot"], 1)
                    t = at(b, j, 2)
                    if t:
                        dve.wait_ge(S["k_out"], t.k + 1)
                        ge(dve, S["logits"], t.k - t.m - 4)
                        for h in range(2):
                            q = slice(64 * h, 64 * h + 64)
                            ins = dve.tensor_copy(QT[q, t.gpar, :, 2 * t.m:2 * t.m + 2, q],
                                                  p_t[q, 0:2 * P].rearrange("p (h w t) -> p h w t", h=2, w=2))
                        ins.then_inc(S["q_out"], 1)
                    if s:
                        dve.wait_ge(S["exp"], s.k + 1)
                        ge(dve, S["pn"], s.k - 1)
                        dve.reciprocal(erec[:, s.par, :], esum[:, s.par, :]).then_inc(S["rec"], 1)
                    if c:
                        dve.wait_ge(S["u"], c.k + 1)
                        dve.wait_ge(S["v_rot"], c.k + 1)
                        ge(dve, S["qkt"], c.k - 1)
                        dve.tensor_tensor(r[:, c.par, :], u[:, c.par, :], v[:, c.par, :], ALU.add).then_inc(S["r"], 1)
                    if a:
                        dve.wait_ge(S["sq"], a.k + 1)
                        ge(dve, S["red"], a.k - 1)
                        dve.tensor_reduce(ssq[:, a.par, :], sq[:, a.par, :].rearrange("p (h f) -> p h f", f=DH), AX.X,
                                          ALU.add).then_inc(S["summed"], 1)
                        dve.wait_ge(S["summed"], a.k + 1)
                        ge(dve, S["rn"], a.k - 1)
                        dve.tensor_scalar(ssqc[:, a.par, :], ssq[:, a.par, :], 1e-24, None, ALU.max).then_inc(S["red"], 1)
                    y = at(b, j, 9)
                    if y and y.pos == STEPS - 1:
                        dve.wait_ge(S["y"], y.batch * G + G)
                        dve.tensor_tensor(tokens(X, y.batch), tokens(X, y.batch), p_y[:, :], ALU.add).then_inc(S["x_out"], 1)

                every_step(dve, step, 10)


ATTENTION_SEMS = ("consts xc weights const_made w_hi w_lo pads rot xt xh xl k_out q_out pt_out v_out o_out o y pn pt exp "
                  "logits r qkt sq qn qk v max red u rec rn v_rot summed x_out").split()


def semaphores(nc, ctx, prefix, names):
    made = {n: ctx.enter_context(nc.semaphore(prefix + n)) for n in names}
    return made, list(made.values())


def clear(nc, sems):
    for s in sems:
        nc.sync.sem_clear(s)
    nc.all_engine_barrier()


def feed_forward(nc, dram, X, ident, banks, w, layer, S):
    with ExitStack() as ctx:
        sb = lambda name, shape, dt=F32: ctx.enter_context(nc.sbuf_tensor("d_" + name, shape, dt))
        w1h, w1l = sb("w1h", [P, 2 * DI], F32R), sb("w1l", [P, 2 * DI], F32R)
        minus_half = sb("minus_half", [P, MT])
        x_cur, xs = sb("x_cur", [P, T]), sb("xs", [P, T])
        st, ag = sb("st", [P, MT, 6]), sb("ag", [P, MT, 2])
        ve, rstd = sb("ve", [P, MT]), sb("rstd", [P, MT])
        xn, xt, xh, xl = sb("xn", [P, T]), sb("xt", [P, T]), sb("xh", [P, T], F32R), sb("xl", [P, T], F32R)
        gate, h, y = sb("gate", [P, NF, T]), sb("h", [P, NF, T]), sb("y", [P, T])
        p_x, p_n, p_h, p_y = banks[0], banks[1], banks[2:6], banks[7]
        p_r = banks[6]

        with nc.Block() as block:

            @block.sync
            def _(sp):
                for dst, src in w.attention_loads(dram, layer):
                    sp.dma_start(dst, src).then_inc(S["weights"], 16)
                sp.dma_start(x_cur[:, :], X[:, 0:T]).then_inc(S["xc"], 16)
                with sp.Fori(1, NB) as b:
                    sp.wait_ge(S["xt"], b)
                    sp.dma_start(x_cur[:, :], tokens(X, b)).then_inc(S["xc"], 16)
                sp.wait_ge(S["weights"], 48)

            @block.tensor
            def _(pe):
                pe.wait_ge(S["w_lo"], 1)

                def first(b):
                    pe.wait_ge(S["xc"], b * 16 + 16)
                    ge(pe, S["xs"], b)
                    for i in range(MT):
                        ins = pe.transpose(p_x[:, i * P:(i + 1) * P], x_cur[:, i * P:(i + 1) * P], ident[:, :])
                    ins.then_inc(S["xt"], 1)

                def back(b):
                    pe.wait_ge(S["xs"], b + 1)
                    ge(pe, S["normed"], b)
                    for i in range(MT):
                        ins = pe.transpose(p_n[:, i * P:(i + 1) * P], xs[:, i * P:(i + 1) * P], ident[:, :])
                    ins.then_inc(S["back"], 1)

                def again(b):
                    pe.wait_ge(S["normed"], b + 1)
                    ge(pe, S["affine"], b)
                    for i in range(MT):
                        ins = pe.transpose(p_r[:, i * P:(i + 1) * P], xn[:, i * P:(i + 1) * P], ident[:, :])
                    ins.then_inc(S["again"], 1)

                def up(b):
                    pe.wait_ge(S["xl"], b + 1)
                    for c, (o, n) in enumerate(FCH):
                        for part in range(2):
                            bank = p_h[2 * (c % 2) + part]
                            if c >= 2:
                                pe.wait_ge(S["h"] if part else S["gate"], NF * b + c - 1)
                            col = slice(DI * (1 - part) + o, DI * (1 - part) + o + n)
                            pe.matmul(bank[0:n, :], w1h[:, col], xh[:, :], start=True, stop=False)
                            pe.matmul(bank[0:n, :], w1l[:, col], xh[:, :], start=False, stop=False)
                            pe.matmul(bank[0:n, :], w1h[:, col], xl[:, :], start=False, stop=True).then_inc(S["up"], 1)

                def down(b):
                    ge(pe, S["x_out"], b)
                    for c, (o, n) in enumerate(FCH):
                        pe.wait_ge(S["h"], b * NF + c + 1)
                        for i in range(MT):
                            ins = pe.matmul(p_y[:, i * P:(i + 1) * P], h[0:n, c, i * P:(i + 1) * P], w.w2[0:n, c, :],
                                            start=(c + i == 0), stop=(c == NF - 1), skip_group_check=True)
                    ins.then_inc(S["down"], 1)

                def step(b, here, before):
                    if here:
                        first(b)
                    if before:
                        up(b - 1)
                    if here:
                        back(b)
                    if before:
                        down(b - 1)
                    if here:
                        again(b)

                step(0, True, False)
                step(1, True, True)
                with pe.Fori(2, NB) as b:
                    step(b, True, True)
                step(NB, False, True)

            @block.scalar
            def _(act):
                act.activation(w1h[:, :], w.w1[:, :], ACT.Copy).then_inc(S["w_hi"], 1)
                act.wait_ge(S["pads"], 1)

                def step(b, here, before):
                    if here:
                        act.wait_ge(S["xt"], b + 1)
                        ge(act, S["back"], b)
                        act.activation(xs[0:64, :], p_x[0:64, :], ACT.Copy)
                        act.activation(xs[64:P, 1:T], p_x[64:P, 0:T - 1], ACT.Copy).then_inc(S["xs"], 1)
                    if before:
                        for c, (o, n) in enumerate(FCH):
                            act.wait_ge(S["up"], (b - 1) * 2 * NF + 2 * c + 1)
                            act.activation(gate[0:n, c, :], p_h[2 * (c % 2)][0:n, :], ACT.Gelu,
                                           bias=w.cols[0:n, 2 + 2 * c:3 + 2 * c]).then_inc(S["gate"], 1)
                    if here:
                        act.wait_ge(S["again"], b + 1)
                        ge(act, S["xl"], b)
                        act.activation(xt[:, :], p_r[:, :], ACT.Identity, scale=w.cols[:, 0:1],
                                       bias=w.cols[:, 1:2]).then_inc(S["affine"], 1)

                step(0, True, False)
                step(1, True, True)
                with act.Fori(2, NB) as b:
                    step(b, True, True)
                step(NB, False, True)

            @block.gpsimd
            def _(pool):
                pool.memset(minus_half[:, :], -0.5).then_inc(S["const_made"], 1)
                pool.wait_ge(S["const_made"], 1)

                def power(b):
                    pool.wait_ge(S["var"], b + 1)
                    pool.tensor_tensor(rstd[:, :], ve[:, :], minus_half[:, :], ALU.pow).then_inc(S["rstd"], 1)

                power(0)
                with pool.Fori(1, NB) as b:
                    power(b)

            @block.vector
            def _(dve):
                dve.memset(xs[:, 0:1], 0.0).then_inc(S["pads"], 1)
                dve.wait_ge(S["w_hi"], 1)
                dve.tensor_tensor(w1l[:, :], w.w1[:, :], w1h[:, :].bitcast(F32), ALU.subtract).then_inc(S["w_lo"], 1)

                def step(b, here, before):
                    if before:
                        for c, (o, n) in enumerate(FCH):
                            dve.wait_ge(S["up"], (b - 1) * 2 * NF + 2 * c + 2)
                            dve.wait_ge(S["gate"], (b - 1) * NF + c + 1)
                            ge(dve, S["down"], b - 1)
                            dve.scalar_tensor_tensor(h[0:n, c, :], p_h[2 * (c % 2) + 1][0:n, :],
                                                     w.cols[0:n, 3 + 2 * c:4 + 2 * c], gate[0:n, c, :], ALU.add,
                                                     ALU.mult).then_inc(S["h"], 1)
                    if here:
                        dve.wait_ge(S["back"], b + 1)
                        ge(dve, S["normed"], b)
                        statistics(dve, p_n, st, ag, ve, S["stats"], S["aggr"], S["var"], b)
                        ge(dve, S["again"], b)
                        normalise(dve, p_n, ag, rstd, S["rstd"], xn[:, :], S["normed"], b)
                    if before:
                        dve.wait_ge(S["down"], b)
                        dve.tensor_tensor(y[:, :].rearrange("p (i d) -> p i d", d=D), p_y[:, :].rearrange("p (i d) -> p i d", d=D),
                                          w.b2[:, :].unsqueeze(1).to_broadcast([P, MT, D]), ALU.add).then_inc(S["x_out"], 1)
                        dve.wait_ge(S["x_out"], b)
                        dve.tensor_tensor(tokens(X, b - 1), tokens(X, b - 1), y[:, :], ALU.add).then_inc(S["x_added"], 1)
                    if here:
                        dve.wait_ge(S["affine"], b + 1)
                        ge(dve, S["up"], b * 2 * NF)
                        dve.tensor_copy(xh[:, :], xt[:, :]).then_inc(S["xh"], 1)
                        dve.wait_ge(S["xh"], b + 1)
                        dve.tensor_tensor(xl[:, :], xt[:, :], xh[:, :].bitcast(F32), ALU.subtract).then_inc(S["xl"], 1)

                step(0, True, False)
                step(1, True, True)
                with dve.Fori(2, NB) as b:
                    step(b, True, True)
                step(NB, False, True)


FEED_FORWARD_SEMS = ("weights xc xt xs back normed again affine xl xh gate h up down w_hi w_lo pads const_made var rstd "
                     "stats aggr x_out x_added").split()


def last_norm(nc, X, X0, out):
    with ExitStack() as ctx:
        sb = lambda name, shape: ctx.enter_context(nc.sbuf_tensor("n_" + name, shape, F32))
        sem = lambda name: ctx.enter_context(nc.semaphore("n_" + name))
        y, x0 = sb("y", [P, NB, T]), sb("x0", [P, NB, T])
        x0_loaded, sum_ready = sem("x0_loaded"), sem("sum_ready")
        st, ag = sb("st", [P, NB, MT, 6]), sb("ag", [P, NB, MT, 2])
        ve, rstd, minus_half = sb("ve", [P, NB, MT]), sb("rstd", [P, NB, MT]), sb("minus_half", [P, MT])
        stats_ready, aggr_ready, var_ready, rstd_ready, y_ready, half_set, stored = (
            sem(n) for n in ("stats_ready", "aggr_ready", "var_ready", "rstd_ready", "y_ready", "half_set", "stored"))
        with nc.Block() as block:

            @block.vector
            def _(dve):
                for b in range(NB + 1):
                    if b < NB:
                        dve.wait_ge(x0_loaded, 16)
                        dve.tensor_tensor(X[:, b * T:(b + 1) * T], X[:, b * T:(b + 1) * T], x0[:, b, :],
                                          ALU.add).then_inc(sum_ready, 1)
                        dve.wait_ge(sum_ready, b + 1)
                        statistics(dve, X[:, b * T:(b + 1) * T], st[:, b], ag[:, b], ve[:, b], stats_ready, aggr_ready, var_ready, b)
                    if b:
                        normalise(dve, X[:, (b - 1) * T:b * T], ag[:, b - 1], rstd[:, b - 1], rstd_ready, y[:, b - 1, :], y_ready, b - 1)

            @block.gpsimd
            def _(pool):
                pool.memset(minus_half[:, :], -0.5).then_inc(half_set, 1)
                pool.wait_ge(half_set, 1)
                for b in range(NB):
                    pool.wait_ge(var_ready, b + 1)
                    pool.tensor_tensor(rstd[:, b, :], ve[:, b, :], minus_half[:, :], ALU.pow).then_inc(rstd_ready, 1)

            @block.sync
            def _(sp):
                sp.dma_start(x0[:, :, :], X0.rearrange("p (b t) -> p b t", b=NB)).then_inc(x0_loaded, 16)
                for b in range(NB):
                    sp.wait_ge(y_ready, b + 1)
                    sp.dma_start(out[:, b * MT:(b + 1) * MT, :], y[:, b, :].rearrange("p (n d) -> p n d", d=D)).then_inc(stored, 16)
                sp.wait_ge(stored, 16 * NB)


def build(nc, dram, out):
    with ExitStack() as ctx:
        X = ctx.enter_context(nc.sbuf_tensor("X", [P, NB * T], F32))
        ident = ctx.enter_context(nc.sbuf_tensor("ident", [P, P], F32))
        banks = [ctx.enter_context(nc.psum_tensor(f"bank{i}", [P, 512], F32)) for i in range(8)]
        X0 = nc.dram_tensor("x0_kept", (P, NB * T), F32).ap()
        ident_loaded = ctx.enter_context(nc.semaphore("ident_loaded"))
        with nc.Block() as block:

            @block.sync
            def _(sp):
                sp.dma_start(ident[:, :], dram["ident"]).then_inc(ident_loaded, 16)
                sp.wait_ge(ident_loaded, 16)

        first_attention(nc, dram, X, ident, banks)
        with ExitStack() as inner:
            w = Weights(nc, inner)
            first_loaded = inner.enter_context(nc.semaphore("first_loaded"))
            kept = inner.enter_context(nc.semaphore("kept"))
            with nc.Block() as block:

                @block.sync
                def _(sp):
                    for dst, src in w.attention_loads(dram, DEPTH - 1):
                        sp.dma_start(dst, src).then_inc(first_loaded, 16)
                    sp.dma_start(X0, X[:, :]).then_inc(kept, 16)
                    sp.wait_ge(first_loaded, 48)
                    sp.wait_ge(kept, 16)

            SA, sa = semaphores(nc, inner, "a_", ATTENTION_SEMS)
            SF, sf = semaphores(nc, inner, "d_", FEED_FORWARD_SEMS)
            with nc.Fori(0, DEPTH) as layer:
                windowed_attention(nc, dram, X, ident, banks, w, layer, SA)
                clear(nc, sa)
                feed_forward(nc, dram, X, ident, banks, w, layer, SF)
                clear(nc, sf)
        last_norm(nc, X, X0, out)


def tables():
    f = np.float32
    i, j = np.arange(P)[:, None], np.arange(P)[None]
    q, k = np.arange(P)[:, None] % 64, np.arange(KW)[None]
    seen = (q <= k) & (k <= q + WIN)
    windows = np.stack([seen & (k >= WIN), seen], 1)
    half = np.arange(0, DH, 2, dtype=f)
    inv = f(1) / f(10000.0) ** (half / f(DH))
    t = np.arange(T, dtype=f)
    freqs = np.concatenate([t[:, None] * inv[None]] * 2, 1)
    base = (half + f(0.4 * DH)) / f(1.4 * DH)
    scale = base[None] ** ((t - f(T // 2)) / f(WIN // 2))[:, None]
    scale = np.concatenate([scale] * 2, 1)
    sign = np.where(np.arange(DH) < DH // 2, f(-1), f(1))
    both = lambda x: np.stack([x * scale * f(8.0), x * (f(1) / scale)], 1).reshape(MT, P, 2, DH).transpose(1, 0, 2, 3)
    return {"ident": np.eye(P, dtype=f), "causal": np.where(i >= j, 0, NEG).astype(f),
            "windows": np.where(windows, 0, NEG).astype(f), "rot_cos": both(np.cos(freqs)).astype(f),
            "rot_sin": both(np.sin(freqs) * sign).astype(f)}


def kernel(**inputs):
    import concourse.bacc as bacc
    from concourse.bass_utils import run_bass_kernel_spmd

    x = {n: np.asarray(a) for n, a in inputs.items()}
    f = "L0_ffn_"
    qkv = x[f + "Wqkv"].reshape(DEPTH, D, 3, G, CQ).transpose(0, 1, 3, 2, 4).reshape(DEPTH, D, G, 3 * CQ)
    wo = x[f + "Wo"].reshape(DEPTH, 8, P, D).transpose(0, 2, 1, 3)
    scales = np.stack([x[f + "q_scale"], x[f + "k_scale"]], 1)
    w2 = np.zeros((DEPTH, NF * P, D), np.float32)
    w2[:, :DI] = x[f + "W2"]
    cols = np.zeros((DEPTH, P, 2 + 2 * NF), np.float32)
    cols[:, :, 0], cols[:, :, 1] = x[f + "ln_g"], x[f + "ln_b"]
    for c, (o, n) in enumerate(FCH):
        cols[:, :n, 2 + 2 * c] = x[f + "b1"][:, DI + o:DI + o + n]
        cols[:, :n, 3 + 2 * c] = x[f + "b1"][:, o:o + n]
    arrays = {
        "x": x["L0_attn_x"].reshape(NB * MT, P, D).transpose(1, 0, 2),
        "pqt": x["L0_attn_P_q"].transpose(2, 0, 1).reshape(DH, H * D),
        "pkt": x["L0_attn_P_k"].transpose(2, 0, 1).reshape(DH, H * D),
        "pv": x["L0_attn_P_v"].transpose(1, 0, 2).reshape(D, H * DH),
        "po": x["L0_attn_P_o"].transpose(0, 2, 1).reshape(8, P, D).transpose(1, 0, 2),
        "qkv": np.roll(qkv, -1, 0), "wo": np.roll(wo, -1, 0), "scales": np.roll(scales, -1, 0),
        "w1": x[f + "W1"], "w2": w2.reshape(DEPTH, NF, P, D).transpose(0, 2, 1, 3), "cols": cols, "b2": x[f + "b2"],
        **tables(),
    }
    arrays = {"in_" + n: np.ascontiguousarray(a) for n, a in arrays.items()}
    nc = bacc.Bacc("TRN2", target_bir_lowering=False, num_devices=1)
    dram = {n[3:]: nc.dram_tensor(n, a.shape, F32, kind="ExternalInput").ap() for n, a in arrays.items()}
    out = nc.dram_tensor("out", (P, NB * MT, D), F32, kind="ExternalOutput").ap()
    build(nc, dram, out)
    r = run_bass_kernel_spmd(nc, [arrays], core_ids=[0])
    got = np.asarray(r.results[0]["out"])
    return np.ascontiguousarray(got.transpose(1, 0, 2)).reshape(NB, T, D)
```

```python
from contextlib import ExitStack

import numpy as np
import concourse.bass as bass
from concourse import mybir

F32 = mybir.dt.float32
F32R = mybir.dt.float32r
BF16 = mybir.dt.bfloat16
ALU = mybir.AluOpType
ACT = mybir.ActivationFunctionType
AX = mybir.AxisListType

NB = 8
T = 512
D = 128
P = 128
MT = T // P
H = 16
DH = 64
DEPTH = 6
WIN = 32
G = 4
HG = H // G
CQ = HG * DH
WP = T // (2 * WIN)
KW = 3 * WIN
XC = WIN + T
DI = int(D * 4 * 2 / 3)
FCH = [(o, min(P, DI - o)) for o in range(0, DI, P)]
NF = len(FCH)
STEPS = H
NEG = -1e30
LN_EPS = 1e-5


def ge(engine, sem, count):
    if isinstance(count, int) and count <= 0:
        return
    engine.wait_ge(sem, count)


class At:

    def __init__(self, b, c):
        self.k = b * STEPS + c
        self.pos = c % STEPS
        self.batch = b + c // STEPS
        self.group = b * G + c // HG
        self.g, self.m = self.pos // MT, self.pos % MT
        self.par, self.gpar = self.pos % 2, self.g % 2


def at(b, j, lag):
    c = j - lag
    if isinstance(b, int) and not 0 <= b * STEPS + c < NB * STEPS:
        return None
    return At(b, c)


def every_step(engine, step, drain):
    for b in range(2):
        for j in range(STEPS):
            step(b, j, b)
    with engine.Fori(1, NB // 2) as i:
        for odd in range(2):
            for j in range(STEPS):
                step(i * 2 + odd, j, odd)
    for j in range(drain):
        step(NB, j, 0)


def tokens(X, batch):
    return X[:, batch * T:(batch + 1) * T] if isinstance(batch, int) else X[:, bass.ts(batch, T)]


def first_attention(nc, dram, X, ident, banks):
    with ExitStack() as ctx:
        sb = lambda name, shape, dt=F32: ctx.enter_context(nc.sbuf_tensor("f_" + name, shape, dt))
        sem = lambda name: ctx.enter_context(nc.semaphore("f_" + name))
        pq_sb, pk_sb = sb("pq_sb", [DH, H * D]), sb("pk_sb", [DH, H * D])
        pv_sb = sb("pv_sb", [P, H * DH])
        po_sb = sb("po_sb", [P, 8, D])
        mh, ml = sb("mh", [P, H, D], F32R), sb("ml", [P, H, D], F32R)
        pvh, pvl = sb("pvh", [P, H * DH], F32R), sb("pvl", [P, H * DH], F32R)
        x_cur = sb("x_cur", [P, T])
        xh, xl = sb("xh", [P, T], F32R), sb("xl", [P, T], F32R)
        yh, yl = sb("yh", [P, 2, T], F32R), sb("yl", [P, 2, T], F32R)
        E = sb("E", [P, 2, MT, T])
        diag_only = sb("diag_only", [P, MT, P])
        ident_b, mask_b, mask_f = sb("ident_b", [P, P], BF16), sb("mask_b", [P, P], BF16), sb("mask_f", [P, P])
        negmax, esum = sb("negmax", [P, 2, MT]), sb("esum", [P, 4, MT])
        ediag, erec = sb("ediag", [P, 2, MT]), sb("erec", [P, 2, MT])
        prob, prob_all = sb("prob", [P, MT, H]), sb("prob_all", [P, MT, H])
        V = sb("V", [P, MT, H * DH])
        O = sb("O", [P, 2, T])
        OT = sb("OT", [P, 2, MT, P])
        xn = sb("xn", [P, T])
        st, ag = sb("st", [P, MT, 6]), sb("ag", [P, MT, 2])
        ve, rstd, mhalf = sb("ve", [P, MT]), sb("rstd", [P, MT]), sb("mhalf", [P, MT])
        p_y, p_s, p_v, p_t, p_z = banks[0], banks[1:5], banks[5], banks[6], banks[7]

        loaded, m_made, w_hi, w_lo, masks_made = (sem(n) for n in ("loaded", "m_made", "w_hi", "w_lo", "masks_made"))
        xc_ready, xt_ready, xh_ready, xl_ready = (sem(n) for n in ("xc_ready", "xt_ready", "xh_ready", "xl_ready"))
        y_ready, yh_ready, yl_ready = (sem(n) for n in ("y_ready", "yh_ready", "yl_ready"))
        logits_ready, max_ready, exp_ready = (sem(n) for n in ("logits_ready", "max_ready", "exp_ready"))
        diag_ready, rec_ready, prob_ready, all_ready = (sem(n) for n in ("diag_ready", "rec_ready", "prob_ready", "all_ready"))
        v_ready, v_out, o_ready, ot_ready, ot_out, z_ready = (sem(n) for n in ("v_ready", "v_out", "o_ready", "ot_ready", "ot_out", "z_ready"))
        sum_ready, stats_ready, aggr_ready, var_ready, rstd_ready, x_out = (sem(n) for n in ("sum_ready", "stats_ready", "aggr_ready", "var_ready", "rstd_ready", "x_out"))
        half_set = sem("half_set")

        with nc.Block() as block:

            @block.sync
            def _(sp):
                for dst, src in ((X[:, :].rearrange("p (n d) -> p n d", d=D), dram["x"]), (pq_sb[:, :], dram["pqt"]),
                                 (pk_sb[:, :], dram["pkt"]), (pv_sb[:, :], dram["pv"]),
                                 (po_sb[:, :, :], dram["po"]), (mask_f[:, :], dram["causal"])):
                    sp.dma_start(dst, src).then_inc(loaded, 16)
                sp.wait_ge(loaded, 96)
                sp.dma_start(x_cur[:, :], X[:, 0:T]).then_inc(xc_ready, 16)
                with sp.Fori(1, NB) as b:
                    sp.wait_ge(xt_ready, b)
                    sp.dma_start(x_cur[:, :], tokens(X, b)).then_inc(xc_ready, 16)

            @block.tensor
            def _(pe):
                pe.wait_ge(loaded, 96)
                for q in range(4):
                    for h in range(4 * q, 4 * q + 4):
                        ins = pe.matmul(p_s[q][:, h % 4 * P:(h % 4 + 1) * P], pq_sb[:, h * D:(h + 1) * D],
                                        pk_sb[:, h * D:(h + 1) * D], start=True, stop=True)
                    ins.then_inc(m_made, 1)
                pe.wait_ge(w_lo, 5)
                pe.wait_ge(masks_made, 2)

                def step(b, j, odd):
                    a = at(b, j, 0)
                    if a and j == 0:
                        pe.wait_ge(xc_ready, b * 16 + 16)
                        ge(pe, ot_out, b * 8 - 8)
                        for i in range(MT):
                            ins = pe.transpose(p_t[:, i * P:(i + 1) * P], x_cur[:, i * P:(i + 1) * P], ident[:, :])
                        ins.then_inc(xt_ready, 1)
                    def logits():
                        s = at(b, j, 1)
                        if s:
                            pe.wait_ge(yl_ready, s.k + 1)
                            for i in range(MT):
                                ge(pe, exp_ready, (s.k - 1) * MT + i + 1)
                                w, q = max(2 * P, (i + 1) * P), slice(i * P, (i + 1) * P)
                                pe.matmul(p_s[i][:, 0:w], yh[:, s.par, q], xh[:, 0:w], start=True, stop=False)
                                pe.matmul(p_s[i][:, 0:w], yl[:, s.par, q], xh[:, 0:w], start=False, stop=False)
                                pe.matmul(p_s[i][:, 0:w], yh[:, s.par, q], xl[:, 0:w], start=False, stop=True)
                                pe.matmul(p_s[i][:, q], ident_b[:, :], mask_b[:, :], start=False, stop=True,
                                          skip_group_check=True).then_inc(logits_ready, 1)

                    def projected():
                        if a:
                            if j == 0:
                                pe.wait_ge(xl_ready, b + 1)
                            ge(pe, yl_ready, a.k)
                            pe.matmul(p_y[:, :], mh[:, a.pos, :], xh[:, :], start=True, stop=False)
                            pe.matmul(p_y[:, :], ml[:, a.pos, :], xh[:, :], start=False, stop=False)
                            pe.matmul(p_y[:, :], mh[:, a.pos, :], xl[:, :], start=False, stop=True).then_inc(y_ready, 1)

                    for stage in (logits, projected) if j == 0 else (projected, logits):
                        stage()
                    if a and j >= 8:
                        i, half = divmod(j - 8, 2)
                        ge(pe, v_out, b * 8 + j - 8)
                        q, c = slice(i * P, (i + 1) * P), slice(half * T, half * T + T)
                        pe.matmul(p_v[:, :], xh[:, q], pvh[:, c], start=True, stop=False)
                        pe.matmul(p_v[:, :], xl[:, q], pvh[:, c], start=False, stop=False)
                        pe.matmul(p_v[:, :], xh[:, q], pvl[:, c], start=False, stop=True).then_inc(v_ready, 1)
                    o = at(b, j, STEPS)
                    if o and 5 <= j < 13:
                        i, half = divmod(j - 5, 2)
                        pe.wait_ge(ot_out, o.batch * 8 + j - 4)
                        if j == 5:
                            ge(pe, sum_ready, o.batch)
                        for c in range(4):
                            ins = pe.matmul(p_z[:, i * P:(i + 1) * P], OT[:, half, c, :], po_sb[:, 4 * half + c, :],
                                            start=(half + c == 0), stop=(half == 1 and c == 3))
                        ins.then_inc(z_ready, 1)
                    if o and 4 <= j < 12:
                        pe.wait_ge(o_ready, o.batch * 8 + j - 3)
                        ge(pe, ot_out, o.batch * 8 + j - 4)
                        if j == 4:
                            pe.wait_ge(xl_ready, NB if isinstance(b, int) and b == NB else o.batch + 2)
                        for c in range(4):
                            ins = pe.transpose(p_t[:, c * P:(c + 1) * P], O[:, j % 2, c * P:(c + 1) * P], ident[:, :])
                        ins.then_inc(ot_ready, 1)

                every_step(pe, step, STEPS)

            @block.scalar
            def _(act):
                act.wait_ge(loaded, 96)
                for q in range(4):
                    act.wait_ge(m_made, q + 1)
                    act.activation(mh[:, 4 * q:4 * q + 4, :], p_s[q][:, :].rearrange("p (a b) -> p a b", a=4),
                                   ACT.Copy, scale=8.0).then_inc(w_hi, 1)
                act.activation(pvh[:, :], pv_sb[:, :], ACT.Copy).then_inc(w_hi, 1)

                def step(b, j, odd):
                    a = at(b, j, 0)
                    if a and j == 0:
                        act.wait_ge(xt_ready, b + 1)
                        ge(act, logits_ready, b * STEPS * MT)
                        ge(act, v_ready, b * 8)
                        act.activation(xh[:, :], p_t[:, :], ACT.Copy).then_inc(xh_ready, 1)
                    if a:
                        act.wait_ge(y_ready, a.k + 1)
                        ge(act, logits_ready, (a.k - 1) * MT)
                        act.activation(yh[:, a.par, :], p_y[:, :], ACT.Copy).then_inc(yh_ready, 1)
                    s = at(b, j, 1)
                    if s:
                        for i in range(MT):
                            act.wait_ge(max_ready, s.k * MT + i + 1)
                            ge(act, diag_ready, (s.k - 2) * MT + i + 1)
                            if i == 0:
                                ge(act, rec_ready, s.k - 3)
                            w = (i + 1) * P
                            act.activation(E[:, s.par, i, 0:w], p_s[i][:, 0:w], ACT.Exp, bias=negmax[:, s.par, i:i + 1],
                                           accum_out=esum[:, s.pos % 4, i:i + 1]).then_inc(exp_ready, 1)
                    if a and j >= 8:
                        i, half = divmod(j - 8, 2)
                        act.wait_ge(v_ready, b * 8 + j - 7)
                        ge(act, o_ready, (b - 1) * 8 + j - 7)
                        act.activation(V[:, i, half * T:half * T + T], p_v[:, :], ACT.Copy).then_inc(v_out, 1)
                    o = at(b, j, STEPS)
                    if o and 4 <= j < 12:
                        act.wait_ge(ot_ready, o.batch * 8 + j - 3)
                        ge(act, z_ready, o.batch * 8 + j - 5)
                        act.activation(OT[:, j % 2, :, :], p_t[:, :].rearrange("p (c t) -> p c t", c=4),
                                       ACT.Copy).then_inc(ot_out, 1)

                every_step(act, step, STEPS)

            @block.gpsimd
            def _(pool):
                pool.memset(mhalf[:, :], -0.5).then_inc(half_set, 1)
                pool.wait_ge(half_set, 1)

                def step(b, j, odd):
                    o = at(b, j, STEPS)
                    if o and 3 <= j < 11:
                        i, half = divmod(j - 3, 2)
                        pool.wait_ge(v_out, o.batch * 8 + j - 2)
                        pool.wait_ge(all_ready, o.batch + 1)
                        ge(pool, ot_ready, o.batch * 8 + j - 4)
                        heads = prob_all[:, i, 8 * half:8 * half + 8].unsqueeze(2).to_broadcast([P, 8, DH])
                        pool.tensor_tensor(O[:, half, :].rearrange("p (h f) -> p h f", f=DH),
                                           V[:, i, half * T:half * T + T].rearrange("p (h f) -> p h f", f=DH),
                                           heads, ALU.mult).then_inc(o_ready, 1)
                    if o and j == 13:
                        pool.wait_ge(var_ready, o.batch + 1)
                        pool.tensor_tensor(rstd[:, :], ve[:, :], mhalf[:, :], ALU.pow).then_inc(rstd_ready, 1)

                every_step(pool, step, STEPS)

            @block.vector
            def _(dve):
                dve.wait_ge(loaded, 96)
                dve.tensor_copy(mask_b[:, :], mask_f[:, :]).then_inc(masks_made, 1)
                dve.tensor_copy(ident_b[:, :], ident[:, :]).then_inc(masks_made, 1)
                for q in range(4):
                    dve.wait_ge(w_hi, q + 1)
                    dve.scalar_tensor_tensor(ml[:, 4 * q:4 * q + 4, :].rearrange("p a b -> p (a b)"), p_s[q][:, :], 8.0,
                                             mh[:, 4 * q:4 * q + 4, :].rearrange("p a b -> p (a b)").bitcast(F32),
                                             ALU.mult, ALU.subtract).then_inc(w_lo, 1)
                dve.wait_ge(w_hi, 5)
                dve.tensor_tensor(pvl[:, :], pv_sb[:, :], pvh[:, :].bitcast(F32), ALU.subtract).then_inc(w_lo, 1)

                def step(b, j, odd):
                    a = at(b, j, 0)
                    if a and j == 0:
                        dve.wait_ge(xh_ready, b + 1)
                        dve.tensor_tensor(xl[:, :], p_t[:, :], xh[:, :].bitcast(F32), ALU.subtract).then_inc(xl_ready, 1)
                    if a:
                        dve.wait_ge(yh_ready, a.k + 1)
                        dve.tensor_tensor(yl[:, a.par, :], p_y[:, :], yh[:, a.par, :].bitcast(F32),
                                          ALU.subtract).then_inc(yl_ready, 1)
                    g = at(b, j, 3)
                    if g:
                        for i in range(MT):
                            dve.wait_ge(exp_ready, g.k * MT + i + 1)
                            if i == 0:
                                ge(dve, prob_ready, g.k - 1)
                            ge(dve, diag_ready, (g.k - 1) * MT + i + 1)
                            dve.scalar_tensor_tensor(diag_only[:, i, :], E[:, g.par, i, i * P:(i + 1) * P], 1.0, ident[:, :], ALU.mult,
                                                     ALU.mult, accum_out=ediag[:, g.par, i:i + 1]).then_inc(diag_ready, 1)
                    s = at(b, j, 1)
                    if s:
                        for i in range(MT):
                            dve.wait_ge(logits_ready, s.k * MT + i + 1)
                            if i == 0:
                                ge(dve, exp_ready, (s.k - 1) * MT)
                            dve.tensor_reduce(negmax[:, s.par, i:i + 1], p_s[i][:, 0:(i + 1) * P], AX.X, ALU.max,
                                              negate=True).then_inc(max_ready, 1)
                    r = at(b, j, 4)
                    if r:
                        dve.reciprocal(erec[:, r.par, :], esum[:, r.pos % 4, :]).then_inc(rec_ready, 1)
                        dve.wait_ge(rec_ready, r.k + 1)
                        dve.wait_ge(diag_ready, (r.k + 1) * MT)
                        dve.tensor_tensor(prob[:, :, r.pos], ediag[:, r.par, :], erec[:, r.par, :],
                                          ALU.mult).then_inc(prob_ready, 1)
                        if r.pos == H - 1:
                            dve.wait_ge(prob_ready, r.k + 1)
                            ge(dve, o_ready, r.batch * 8)
                            dve.tensor_copy(prob_all[:, :, :], prob[:, :, :]).then_inc(all_ready, 1)
                    o = at(b, j, STEPS)
                    if o and j == 13:
                        dve.wait_ge(z_ready, (o.batch + 1) * 8)
                        ge(dve, x_out, o.batch)
                        dve.tensor_tensor(xn[:, :], tokens(X, o.batch), p_z[:, :], ALU.add).then_inc(sum_ready, 1)
                        dve.wait_ge(sum_ready, o.batch + 1)
                        statistics(dve, xn, st, ag, ve, stats_ready, aggr_ready, var_ready, o.batch)
                    if o and j == 14:
                        normalise(dve, xn, ag, rstd, rstd_ready, tokens(X, o.batch), x_out, o.batch)

                every_step(dve, step, STEPS)


def statistics(dve, x, st, ag, ve, stats_ready, aggr_ready, var_ready, n):
    for i in range(MT):
        ins = dve.bn_stats(st[:, i, :], x[:, i * D:(i + 1) * D])
    ins.then_inc(stats_ready, 1)
    dve.wait_ge(stats_ready, n + 1)
    dve.memset(ve[:, :], 0.0)
    for i in range(MT):
        ins = dve.bn_aggr(ag[:, i, :], st[:, i, :])
    ins.then_inc(aggr_ready, 1)
    dve.wait_ge(aggr_ready, n + 1)
    dve.tensor_scalar(ve[:, :], ag[:, :, 1], LN_EPS, None, ALU.add).then_inc(var_ready, 1)


def normalise(dve, x, ag, rstd, rstd_ready, out, done, n):
    dve.wait_ge(rstd_ready, n + 1)
    for i in range(MT):
        ins = dve.tensor_scalar(out[:, i * D:(i + 1) * D], x[:, i * D:(i + 1) * D], ag[:, i, 0:1], rstd[:, i:i + 1],
                                ALU.subtract, ALU.mult)
    ins.then_inc(done, 1)


class Weights:

    def __init__(self, nc, ctx):
        sb = lambda name, shape: ctx.enter_context(nc.sbuf_tensor(name, shape, F32))
        self.qkv = sb("w_qkv", [P, G, 3 * CQ])
        self.scales = sb("w_scales", [P, 2, DH])
        self.out = sb("w_out", [P, 8, D])
        self.w1 = sb("w_w1", [P, 2 * DI])
        self.w2 = sb("w_w2", [P, NF, D])
        self.cols = sb("w_cols", [P, 2 + 2 * NF])
        self.b2 = sb("w_b2", [P, D])

    def attention_loads(self, dram, layer):
        return ((self.qkv[:, :, :], dram["qkv"][layer]), (self.out[:, :, :], dram["wo"][layer]),
                (self.scales[:, :, :], dram["scales"][layer].partition_broadcast(P)))

    def feed_forward_loads(self, dram, layer):
        return ((self.w1[:, :], dram["w1"][layer]), (self.w2[:, :, :], dram["w2"][layer]),
                (self.cols[:, :], dram["cols"][layer]), (self.b2[:, :], dram["b2"][layer].partition_broadcast(P)))


LAG_R, LAG_A, LAG_T, LAG_S, LAG_E, LAG_PT, LAG_O, LAG_Y = 1, 2, 3, 7, 8, 10, 11, 12


def attention_buffers(nc, ctx):
    made = {}

    def sb(name, shape, dt=F32):
        made[name] = ctx.enter_context(nc.sbuf_tensor("a_" + name, shape, dt))

    for n in ("wh", "wl"):
        sb(n, [P, G, 3 * CQ], F32R)
    for n in ("tabs_c", "tabs_s", "rot_c", "rot_s"):
        sb(n, [P, MT, 2, DH])
    sb("masks_f", [P, 2, 4 * KW])
    sb("masks", [P, 2, 4 * KW], F32R)
    sb("ident_r", [P, P], F32R)
    sb("minus_half", [P, 2 * HG])
    sb("x_cur", [P, T])
    for n in ("xh", "xl"):
        sb(n, [P, 2, XC], F32R)
    sb("sq", [P, 2 * CQ])
    for n in ("ssq", "ssqc", "rn"):
        sb(n, [P, 2, 2 * HG])
    for n in ("qn", "u", "v", "r"):
        sb(n, [P, 2, 2 * CQ])
    sb("QT", [P, 2, 2, WP, P])
    sb("KT", [P, 2, 2, XC])
    sb("V", [KW, G, WP, CQ])
    sb("E", [P, 2, 4, KW])
    sb("PN", [P, 2, 4, KW])
    for n in ("negmax", "esum", "erec"):
        sb(n, [P, 2, 4])
    sb("PT", [KW, 2, 4, P])
    sb("OT", [P, 2, 2, T])
    return made


def attention_constants(nc, dram, ctx, A, ident):
    sem = lambda name: ctx.enter_context(nc.semaphore("c_" + name))
    loaded, zeroed, made = sem("loaded"), sem("zeroed"), sem("made")
    with nc.Block() as block:

        @block.sync
        def _(sp):
            for dst, src in ((A["tabs_c"][:, :, :, :], "rot_cos"), (A["tabs_s"][:, :, :, :], "rot_sin"),
                             (A["masks_f"][:, :, :], "windows")):
                sp.dma_start(dst, dram[src]).then_inc(loaded, 16)

        @block.gpsimd
        def _(pool):
            pool.memset(A["minus_half"][:, :], -0.5).then_inc(zeroed, 1)
            pool.memset(A["QT"][:, :, :, :, :], 0.0).then_inc(zeroed, 1)
            pool.memset(A["KT"][:, :, :, 0:WIN], 0.0).then_inc(zeroed, 1)
            pool.wait_ge(zeroed, 3)

        @block.vector
        def _(dve):
            for n in ("xh", "xl"):
                dve.memset(A[n][:, :, 0:WIN + 2].bitcast(F32), 0.0).then_inc(made, 1)
            dve.tensor_copy(A["ident_r"][:, :], ident[:, :]).then_inc(made, 1)
            dve.wait_ge(loaded, 48)
            dve.tensor_copy(A["masks"][:, :, :], A["masks_f"][:, :, :]).then_inc(made, 1)
            dve.wait_ge(made, 4)


def split_attention_weights(A, w, S, act=None, dve=None):
    if act:
        for g in range(G):
            act.activation(A["wh"][:, g, :], w.qkv[:, g, :], ACT.Copy).then_inc(S["aw_hi"], 1)
    if dve:
        rot_c, rot_s, tabs_c, tabs_s = A["rot_c"], A["rot_s"], A["tabs_c"], A["tabs_s"]
        for g in range(G):
            dve.wait_ge(S["aw_hi"], g + 1)
            dve.tensor_tensor(A["wl"][:, g, :], w.qkv[:, g, :], A["wh"][:, g, :].bitcast(F32), ALU.subtract)
        dve.tensor_tensor(rot_c[:, :, :, :].rearrange("p m s f -> p m (s f)"),
                          tabs_c[:, :, :, :].rearrange("p m s f -> p m (s f)"),
                          w.scales[:, :, :].rearrange("p s f -> p (s f)").unsqueeze(1).to_broadcast([P, MT, 2 * DH]),
                          ALU.mult)
        swap = lambda x: x.rearrange("p s (h f) -> p s h f", h=2)
        for m in range(MT):
            dve.tensor_tensor(swap(rot_s[:, m, :, :]), swap(tabs_s[:, m, :, :]), swap(w.scales[:, :, :])[:, :, ::-1, :],
                              ALU.mult)


def windowed_attention(nc, X, ident, banks, A, w, dram, layer, S):
    wh, wl, rot_c, rot_s, masks, ident_r, minus_half = (
        A[n] for n in ("wh", "wl", "rot_c", "rot_s", "masks", "ident_r", "minus_half"))
    x_cur, xh, xl, sq, ssq, ssqc, rn, qn, u, v, r = (
        A[n] for n in ("x_cur", "xh", "xl", "sq", "ssq", "ssqc", "rn", "qn", "u", "v", "r"))
    QT, KT, V, E, PN, negmax, esum, erec, PT, OT = (
        A[n] for n in ("QT", "KT", "V", "E", "PN", "negmax", "esum", "erec", "PT", "OT"))
    p_qk, p_v, p_t, p_s, p_p, p_o, p_y = banks[0:2], banks[2], banks[3], banks[4], banks[5], banks[6], banks[7]
    with nc.Block() as block:

        @block.sync
        def _(sp):
            sp.dma_start(x_cur[:, :], X[:, 0:T]).then_inc(S["xc"], 16)
            for dst, src in w.feed_forward_loads(dram, layer):
                sp.dma_start(dst, src).then_inc(S["weights"], 16)
            with sp.Fori(1, NB) as b:
                sp.wait_ge(S["xt"], b)
                sp.dma_start(x_cur[:, :], tokens(X, b)).then_inc(S["xc"], 16)
            sp.wait_ge(S["weights"], 64)

        @block.tensor
        def _(pe):
            def step(b, j, odd):
                a = at(b, j, 0)
                if a and j == 0:
                    pe.wait_ge(S["xc"], b * 16 + 16)
                    ge(pe, S["k_out"], a.k - LAG_T)
                    ge(pe, S["q_out"], a.k - LAG_T)
                    for i in range(MT):
                        ins = pe.transpose(p_t[:, i * P:(i + 1) * P], x_cur[:, i * P:(i + 1) * P], ident[:, :])
                    ins.then_inc(S["xt"], 1)
                def project():
                    if a:
                        if j == 0:
                            pe.wait_ge(S["xl"], b + 1)
                        ge(pe, S["sq"], a.k - 1)
                        ge(pe, S["qn"], a.k - 1)
                        m, g = slice(WIN + a.m * P, WIN + (a.m + 1) * P), a.g
                        pe.matmul(p_qk[a.par][:, :], xh[:, odd, m], wh[:, g, 0:2 * CQ], start=True, stop=False)
                        pe.matmul(p_qk[a.par][:, :], xl[:, odd, m], wh[:, g, 0:2 * CQ], start=False, stop=False)
                        pe.matmul(p_qk[a.par][:, :], xh[:, odd, m], wl[:, g, 0:2 * CQ], start=False, stop=True).then_inc(S["qk"], 1)

                def values():
                    if a:
                        g = a.g
                        ge(pe, S["v_out"], a.k)
                        for n in range(2):
                            m = slice(64 * (2 * a.m + n), 64 * (2 * a.m + n) + KW)
                            to, c = p_v[0:KW, n * CQ:(n + 1) * CQ], slice(2 * CQ, 3 * CQ)
                            pe.matmul(to, xh[:, odd, m], wh[:, g, c], start=True, stop=False)
                            pe.matmul(to, xl[:, odd, m], wh[:, g, c], start=False, stop=False)
                            ins = pe.matmul(to, xh[:, odd, m], wl[:, g, c], start=False, stop=True)
                        ins.then_inc(S["v"], 1)

                def behind():
                    o = at(b, j, LAG_O)
                    if o:
                        pe.wait_ge(S["pt_out"], o.k + 1)
                        pe.wait_ge(S["v_out"], o.k - o.m + 4)
                        ge(pe, S["o_out"], o.k)
                        hp, half = divmod(o.m, 2)
                        for n in range(4):
                            ins = pe.matmul(p_o[:, n * P:(n + 1) * P], V[:, o.g, 4 * half + n, hp * P:(hp + 1) * P],
                                            PT[:, o.par, n, :], start=True, stop=True)
                        ins.then_inc(S["o"], 1)
                    y = at(b, j, LAG_Y)
                    if y and y.m == 3:
                        pe.wait_ge(S["o_out"], y.k + 1)
                        if y.g == 0:
                            ge(pe, S["x_out"], y.batch)
                        for i in range(MT):
                            for hp in range(2):
                                ins = pe.matmul(p_y[:, i * P:(i + 1) * P], OT[:, y.gpar, hp, i * P:(i + 1) * P],
                                                w.out[:, 2 * y.g + hp, :], start=(y.g + i + hp == 0),
                                                stop=(y.g == G - 1 and hp == 1), skip_group_check=True)
                        ins.then_inc(S["y"], 1)
                    t = at(b, j, LAG_PT)
                    if t:
                        pe.wait_ge(S["pn"], t.k + 1)
                        ge(pe, S["pt_out"], t.k)
                        for n in range(4):
                            ins = pe.transpose(p_p[0:KW, n * P:(n + 1) * P], PN[:, t.par, n, :], ident[:, :])
                        ins.then_inc(S["pt"], 1)
                    t = at(b, j, LAG_T)
                    if t:
                        pe.wait_ge(S["r"], t.k + 1)
                        ge(pe, S["k_out"], t.k)
                        ge(pe, S["q_out"], t.k)
                        if t.pos == STEPS - LAG_T:
                            pe.wait_ge(S["xl"], NB if isinstance(b, int) and b == NB else t.batch + 2)
                        for c in range(4):
                            ins = pe.transpose(p_t[:, c * P:(c + 1) * P], r[:, t.par, c * P:(c + 1) * P], ident[:, :])
                        ins.then_inc(S["qkt"], 1)
                    s = at(b, j, LAG_S)
                    if s:
                        pe.wait_ge(S["k_out"], s.k - s.m + 4)
                        pe.wait_ge(S["q_out"], s.k - s.m + 4)
                        ge(pe, S["exp"], s.k)
                        hp, half = divmod(s.m, 2)
                        pe.matmul(p_s[:, 0:4 * KW], ident_r[:, :], masks[:, int(half > 0), :], start=True, stop=True)
                        for n in range(4):
                            first = 64 * (4 * half + n)
                            ins = pe.matmul(p_s[:, n * KW:(n + 1) * KW], QT[:, s.gpar, hp, 4 * half + n, :],
                                            KT[:, s.gpar, hp, first:first + KW], start=False, stop=True,
                                            skip_group_check=True)
                        ins.then_inc(S["logits"], 1)

                for stage in (behind, project, values) if j == 0 else (project, behind, values):
                    stage()

            every_step(pe, step, LAG_Y + 1)

        @block.scalar
        def _(act):
            def step(b, j, odd):
                a = at(b, j, 0)
                if a and j == 0:
                    act.wait_ge(S["xt"], b + 1)
                    ge(act, S["v"], a.k - STEPS)
                    act.activation(xh[0:64, odd, WIN:XC], p_t[0:64, :], ACT.Copy)
                    act.activation(xh[64:P, odd, WIN + 1:XC], p_t[64:P, 0:T - 1], ACT.Copy).then_inc(S["xh"], 1)
                v_ = at(b, j, 1)
                if v_:
                    act.wait_ge(S["v"], v_.k + 1)
                    ge(act, S["o"], v_.k - v_.m - 12)
                    act.activation(V[:, v_.g, 2 * v_.m:2 * v_.m + 2, :],
                                   p_v[0:KW, :].rearrange("p (n c) -> p n c", n=2), ACT.Copy).then_inc(S["v_out"], 1)
                def squares():
                    if a:
                        act.wait_ge(S["qk"], a.k + 1)
                        ge(act, S["summed"], a.k)
                        act.activation(sq[:, :], p_qk[a.par][:, :], ACT.Square).then_inc(S["sq"], 1)

                if j:
                    squares()
                s = at(b, j, LAG_E)
                if s:
                    act.wait_ge(S["max"], s.k + 1)
                    ge(act, S["pn"], s.k - 1)
                    for n in range(4):
                        ins = act.activation(E[:, s.par, n, :], p_s[:, n * KW:(n + 1) * KW], ACT.Exp,
                                             bias=negmax[:, s.par, n:n + 1], accum_out=esum[:, s.par, n:n + 1])
                    ins.then_inc(S["exp"], 1)
                o = at(b, j, LAG_O)
                if o:
                    act.wait_ge(S["o"], o.k + 1)
                    ge(act, S["y"], o.group - 1)
                    hp, half = divmod(o.m, 2)
                    for h in range(2):
                        q = slice(64 * h, 64 * h + 64)
                        ins = act.activation(
                            OT[q, o.gpar, hp, 4 * 64 * half:4 * 64 * (half + 1)].rearrange("p (n t) -> p n t", n=4),
                            p_o[q, :].rearrange("p (n h t) -> p n h t", n=4, h=2)[:, :, h, :], ACT.Copy)
                    ins.then_inc(S["o_out"], 1)
                t = at(b, j, LAG_PT)
                if t:
                    act.wait_ge(S["pt"], t.k + 1)
                    ge(act, S["o"], t.k - 1)
                    act.activation(PT[:, t.par, :, :], p_p[0:KW, :].rearrange("p (n q) -> p n q", n=4),
                                   ACT.Copy).then_inc(S["pt_out"], 1)
                t = at(b, j, LAG_T)
                if t:
                    act.wait_ge(S["qkt"], t.k + 1)
                    ge(act, S["logits"], t.k - t.m - 4)
                    c = WIN + t.m * P
                    act.activation(KT[:, t.gpar, :, c:c + P], p_t[:, 2 * P:].rearrange("p (h t) -> p h t", h=2),
                                   ACT.Copy).then_inc(S["k_out"], 1)
                if j == 0:
                    squares()

            every_step(act, step, LAG_Y + 1)

        @block.gpsimd
        def _(pool):
            def step(b, j, odd):
                a = at(b, j, LAG_R)
                if a:
                    pool.wait_ge(S["qn"], a.k + 1)
                    ge(pool, S["r"], a.k - 1)
                    view = lambda x: x[:, a.par, :].rearrange("p (s h f) -> p s h f", s=2, h=HG)
                    tab = rot_c[:, a.m, :, :].unsqueeze(2).to_broadcast([P, 2, HG, DH])
                    pool.tensor_tensor(view(u), view(qn), tab, ALU.mult).then_inc(S["u"], 1)
                a = at(b, j, 0)
                if a:
                    pool.wait_ge(S["red"], a.k + 1)
                    ge(pool, S["qn"], a.k - 1)
                    pool.tensor_tensor(rn[:, a.par, :], ssqc[:, a.par, :], minus_half[:, :], ALU.pow).then_inc(S["rn"], 1)
                s = at(b, j, LAG_E)
                if s:
                    pool.wait_ge(S["rec"], s.k + 1)
                    ge(pool, S["pt"], s.k - 1)
                    pool.tensor_tensor(PN[:, s.par, :, :], E[:, s.par, :, :],
                                       erec[:, s.par, :].unsqueeze(2).to_broadcast([P, 4, KW]),
                                       ALU.mult).then_inc(S["pn"], 1)

            every_step(pool, step, LAG_Y + 1)

        @block.vector
        def _(dve):
            def step(b, j, odd):
                a = at(b, j, 0)
                if a and j == 0:
                    dve.wait_ge(S["xh"], b + 1)
                    dve.tensor_tensor(xl[0:64, odd, WIN:XC], p_t[0:64, :], xh[0:64, odd, WIN:XC].bitcast(F32), ALU.subtract)
                    dve.tensor_tensor(xl[64:P, odd, WIN + 1:XC], p_t[64:P, 0:T - 1], xh[64:P, odd, WIN + 1:XC].bitcast(F32),
                                      ALU.subtract).then_inc(S["xl"], 1)
                s = at(b, j, LAG_E)
                if s:
                    dve.wait_ge(S["logits"], s.k + 1)
                    ge(dve, S["exp"], s.k - 1)
                    dve.tensor_reduce(negmax[:, s.par, :], p_s[:, 0:4 * KW].rearrange("p (n k) -> p n k", n=4), AX.X,
                                      ALU.max, negate=True).then_inc(S["max"], 1)
                c = at(b, j, LAG_A)
                if c:
                    dve.wait_ge(S["u"], c.k + 1)
                    dve.wait_ge(S["v_rot"], c.k + 1)
                    ge(dve, S["qkt"], c.k - 1)
                    dve.tensor_tensor(r[:, c.par, :], u[:, c.par, :], v[:, c.par, :], ALU.add).then_inc(S["r"], 1)
                c = at(b, j, LAG_R)
                if c:
                    dve.wait_ge(S["rn"], c.k + 1)
                    ge(dve, S["u"], c.k - 1)
                    ge(dve, S["v_rot"], c.k - 1)
                    heads = lambda x: x.rearrange("p (h f) -> p h f", f=DH)
                    dve.tensor_tensor(heads(qn[:, c.par, :]), heads(p_qk[c.par][:, :]),
                                      rn[:, c.par, :].unsqueeze(2).to_broadcast([P, 2 * HG, DH]),
                                      ALU.mult).then_inc(S["qn"], 1)
                    dve.wait_ge(S["qn"], c.k + 1)
                    ge(dve, S["r"], c.k - 1)
                    halves = lambda x: x.rearrange("p (s h t f) -> p s h t f", s=2, h=HG, t=2)
                    tab = rot_s[:, c.m, :, :].rearrange("p s (t f) -> p s t f", t=2).unsqueeze(2).to_broadcast([P, 2, HG, 2, DH // 2])
                    dve.tensor_tensor(halves(v[:, c.par, :]), halves(qn[:, c.par, :])[:, :, :, ::-1, :], tab,
                                      ALU.mult).then_inc(S["v_rot"], 1)
                if a:
                    dve.wait_ge(S["sq"], a.k + 1)
                    ge(dve, S["red"], a.k - 1)
                    dve.tensor_reduce(ssq[:, a.par, :], sq[:, :].rearrange("p (h f) -> p h f", f=DH), AX.X,
                                      ALU.add).then_inc(S["summed"], 1)
                    dve.wait_ge(S["summed"], a.k + 1)
                    ge(dve, S["rn"], a.k - 1)
                    dve.tensor_scalar(ssqc[:, a.par, :], ssq[:, a.par, :], 1e-24, None, ALU.max).then_inc(S["red"], 1)
                t = at(b, j, LAG_T)
                if t:
                    dve.wait_ge(S["k_out"], t.k + 1)
                    ge(dve, S["logits"], t.k - t.m - 4)
                    for h in range(2):
                        q = slice(64 * h, 64 * h + 64)
                        ins = dve.tensor_copy(QT[q, t.gpar, :, 2 * t.m:2 * t.m + 2, q],
                                              p_t[q, 0:2 * P].rearrange("p (h w t) -> p h w t", h=2, w=2))
                    ins.then_inc(S["q_out"], 1)
                if s:
                    dve.wait_ge(S["exp"], s.k + 1)
                    ge(dve, S["pn"], s.k - 1)
                    dve.reciprocal(erec[:, s.par, :], esum[:, s.par, :]).then_inc(S["rec"], 1)
                y = at(b, j, LAG_Y)
                if y and y.pos == STEPS - 1:
                    dve.wait_ge(S["y"], y.batch * G + G)
                    dve.tensor_tensor(tokens(X, y.batch), tokens(X, y.batch), p_y[:, :], ALU.add).then_inc(S["x_out"], 1)

            every_step(dve, step, LAG_Y + 1)


ATTENTION_SEMS = ("xc weights xt xh xl k_out q_out pt_out v_out o_out o y pn pt exp "
                  "logits r qkt sq qn qk v max red u rec rn v_rot summed x_out").split()


def semaphores(nc, ctx, prefix, names):
    made = {n: ctx.enter_context(nc.semaphore(prefix + n)) for n in names}
    return made, list(made.values())


def clear(nc, sems):
    for s in sems:
        nc.sync.sem_clear(s)
    nc.all_engine_barrier()


def feed_forward(nc, dram, X, ident, banks, A, w, layer, S):
    with ExitStack() as ctx:
        sb = lambda name, shape, dt=F32: ctx.enter_context(nc.sbuf_tensor("d_" + name, shape, dt))
        w1h, w1l = sb("w1h", [P, 2 * DI], F32R), sb("w1l", [P, 2 * DI], F32R)
        minus_half = sb("minus_half", [P, MT])
        x_cur, y = A["x_cur"], A["sq"]
        xs, xn = A["v"][:, 0, :], A["r"][:, 0, :]
        st, ag = sb("st", [P, MT, 6]), sb("ag", [P, MT, 2])
        ve, rstd = sb("ve", [P, MT]), sb("rstd", [P, MT])
        xt, xh, xl = sb("xt", [P, T]), sb("xh", [P, T], F32R), sb("xl", [P, T], F32R)
        gate, h = sb("gate", [P, NF, T]), sb("h", [P, NF, T])
        p_x, p_n, p_h, p_y = banks[0], banks[1], banks[2:6], banks[7]
        p_r = banks[6]

        with nc.Block() as block:

            @block.sync
            def _(sp):
                for dst, src in w.attention_loads(dram, layer):
                    sp.dma_start(dst, src).then_inc(S["weights"], 16)
                sp.dma_start(x_cur[:, :], X[:, 0:T]).then_inc(S["xc"], 16)
                with sp.Fori(1, NB) as b:
                    sp.wait_ge(S["xt"], b)
                    sp.dma_start(x_cur[:, :], tokens(X, b)).then_inc(S["xc"], 16)

            @block.tensor
            def _(pe):
                pe.wait_ge(S["w_lo"], 1)

                def first(b):
                    pe.wait_ge(S["xc"], b * 16 + 16)
                    ge(pe, S["xs"], b)
                    for i in range(MT):
                        ins = pe.transpose(p_x[:, i * P:(i + 1) * P], x_cur[:, i * P:(i + 1) * P], ident[:, :])
                    ins.then_inc(S["xt"], 1)

                def back(b):
                    pe.wait_ge(S["xs"], b + 1)
                    ge(pe, S["normed"], b)
                    for i in range(MT):
                        ins = pe.transpose(p_n[:, i * P:(i + 1) * P], xs[:, i * P:(i + 1) * P], ident[:, :])
                    ins.then_inc(S["back"], 1)

                def again(b):
                    pe.wait_ge(S["normed"], b + 1)
                    ge(pe, S["affine"], b)
                    for i in range(MT):
                        ins = pe.transpose(p_r[:, i * P:(i + 1) * P], xn[:, i * P:(i + 1) * P], ident[:, :])
                    ins.then_inc(S["again"], 1)

                def up(b):
                    pe.wait_ge(S["xl"], b + 1)
                    for c, (o, n) in enumerate(FCH):
                        for part in range(2):
                            bank = p_h[2 * (c % 2) + part]
                            if c >= 2:
                                pe.wait_ge(S["h"] if part else S["gate"], NF * b + c - 1)
                            col = slice(DI * (1 - part) + o, DI * (1 - part) + o + n)
                            pe.matmul(bank[0:n, :], w1h[:, col], xh[:, :], start=True, stop=False)
                            pe.matmul(bank[0:n, :], w1l[:, col], xh[:, :], start=False, stop=False)
                            pe.matmul(bank[0:n, :], w1h[:, col], xl[:, :], start=False, stop=True).then_inc(S["up"], 1)

                def down(b):
                    ge(pe, S["x_out"], b)
                    for c, (o, n) in enumerate(FCH):
                        pe.wait_ge(S["h"], b * NF + c + 1)
                        for i in range(MT):
                            ins = pe.matmul(p_y[:, i * P:(i + 1) * P], h[0:n, c, i * P:(i + 1) * P], w.w2[0:n, c, :],
                                            start=(c + i == 0), stop=(c == NF - 1), skip_group_check=True)
                    ins.then_inc(S["down"], 1)

                def step(b, here, before):
                    if here:
                        first(b)
                    if before:
                        up(b - 1)
                    if here:
                        back(b)
                    if before:
                        down(b - 1)
                    if here:
                        again(b)

                step(0, True, False)
                step(1, True, True)
                with pe.Fori(2, NB) as b:
                    step(b, True, True)
                step(NB, False, True)

            @block.scalar
            def _(act):
                act.activation(w1h[:, :], w.w1[:, :], ACT.Copy).then_inc(S["w_hi"], 1)
                act.wait_ge(S["pads"], 1)

                def step(b, here, before):
                    if here:
                        act.wait_ge(S["xt"], b + 1)
                        ge(act, S["back"], b)
                        act.activation(xs[0:64, :], p_x[0:64, :], ACT.Copy)
                        act.activation(xs[64:P, 1:T], p_x[64:P, 0:T - 1], ACT.Copy).then_inc(S["xs"], 1)
                    if before:
                        for c, (o, n) in enumerate(FCH):
                            act.wait_ge(S["up"], (b - 1) * 2 * NF + 2 * c + 1)
                            act.activation(gate[0:n, c, :], p_h[2 * (c % 2)][0:n, :], ACT.Gelu,
                                           bias=w.cols[0:n, 2 + 2 * c:3 + 2 * c]).then_inc(S["gate"], 1)
                    if here:
                        act.wait_ge(S["again"], b + 1)
                        ge(act, S["xl"], b)
                        act.activation(xt[:, :], p_r[:, :], ACT.Identity, scale=w.cols[:, 0:1],
                                       bias=w.cols[:, 1:2]).then_inc(S["affine"], 1)

                step(0, True, False)
                step(1, True, True)
                with act.Fori(2, NB) as b:
                    step(b, True, True)
                step(NB, False, True)
                act.wait_ge(S["weights"], 48)
                split_attention_weights(A, w, S, act=act)

            @block.gpsimd
            def _(pool):
                pool.memset(minus_half[:, :], -0.5).then_inc(S["const_made"], 1)
                pool.wait_ge(S["const_made"], 1)

                def power(b):
                    pool.wait_ge(S["var"], b + 1)
                    pool.tensor_tensor(rstd[:, :], ve[:, :], minus_half[:, :], ALU.pow).then_inc(S["rstd"], 1)

                power(0)
                with pool.Fori(1, NB) as b:
                    power(b)

            @block.vector
            def _(dve):
                dve.memset(xs[:, 0:1], 0.0).then_inc(S["pads"], 1)
                dve.wait_ge(S["w_hi"], 1)
                dve.tensor_tensor(w1l[:, :], w.w1[:, :], w1h[:, :].bitcast(F32), ALU.subtract).then_inc(S["w_lo"], 1)

                def step(b, here, before):
                    if before:
                        for c, (o, n) in enumerate(FCH):
                            dve.wait_ge(S["up"], (b - 1) * 2 * NF + 2 * c + 2)
                            dve.wait_ge(S["gate"], (b - 1) * NF + c + 1)
                            ge(dve, S["down"], b - 1)
                            dve.scalar_tensor_tensor(h[0:n, c, :], p_h[2 * (c % 2) + 1][0:n, :],
                                                     w.cols[0:n, 3 + 2 * c:4 + 2 * c], gate[0:n, c, :], ALU.add,
                                                     ALU.mult).then_inc(S["h"], 1)
                    if here:
                        dve.wait_ge(S["back"], b + 1)
                        ge(dve, S["normed"], b)
                        statistics(dve, p_n, st, ag, ve, S["stats"], S["aggr"], S["var"], b)
                        ge(dve, S["again"], b)
                        normalise(dve, p_n, ag, rstd, S["rstd"], xn[:, :], S["normed"], b)
                    if before:
                        dve.wait_ge(S["down"], b)
                        dve.tensor_tensor(y[:, :].rearrange("p (i d) -> p i d", d=D), p_y[:, :].rearrange("p (i d) -> p i d", d=D),
                                          w.b2[:, :].unsqueeze(1).to_broadcast([P, MT, D]), ALU.add).then_inc(S["x_out"], 1)
                        dve.wait_ge(S["x_out"], b)
                        dve.tensor_tensor(tokens(X, b - 1), tokens(X, b - 1), y[:, :], ALU.add).then_inc(S["x_added"], 1)
                    if here:
                        dve.wait_ge(S["affine"], b + 1)
                        ge(dve, S["up"], b * 2 * NF)
                        dve.tensor_copy(xh[:, :], xt[:, :]).then_inc(S["xh"], 1)
                        dve.wait_ge(S["xh"], b + 1)
                        dve.tensor_tensor(xl[:, :], xt[:, :], xh[:, :].bitcast(F32), ALU.subtract).then_inc(S["xl"], 1)

                step(0, True, False)
                step(1, True, True)
                with dve.Fori(2, NB) as b:
                    step(b, True, True)
                dve.wait_ge(S["weights"], 48)
                split_attention_weights(A, w, S, dve=dve)
                step(NB, False, True)


FEED_FORWARD_SEMS = ("aw_hi weights xc xt xs back normed again affine xl xh gate h up down w_hi w_lo pads const_made var rstd "
                     "stats aggr x_out x_added").split()


def last_norm(nc, X, X0, out):
    with ExitStack() as ctx:
        sb = lambda name, shape: ctx.enter_context(nc.sbuf_tensor("n_" + name, shape, F32))
        sem = lambda name: ctx.enter_context(nc.semaphore("n_" + name))
        y, x0 = sb("y", [P, NB, T]), sb("x0", [P, NB, T])
        x0_loaded, sum_ready = sem("x0_loaded"), sem("sum_ready")
        st, ag = sb("st", [P, NB, MT, 6]), sb("ag", [P, NB, MT, 2])
        ve, rstd, minus_half = sb("ve", [P, NB, MT]), sb("rstd", [P, NB, MT]), sb("minus_half", [P, MT])
        stats_ready, aggr_ready, var_ready, rstd_ready, y_ready, half_set, stored = (
            sem(n) for n in ("stats_ready", "aggr_ready", "var_ready", "rstd_ready", "y_ready", "half_set", "stored"))
        with nc.Block() as block:

            @block.vector
            def _(dve):
                for b in range(NB + 1):
                    if b < NB:
                        dve.wait_ge(x0_loaded, 16)
                        dve.tensor_tensor(X[:, b * T:(b + 1) * T], X[:, b * T:(b + 1) * T], x0[:, b, :],
                                          ALU.add).then_inc(sum_ready, 1)
                        dve.wait_ge(sum_ready, b + 1)
                        statistics(dve, X[:, b * T:(b + 1) * T], st[:, b], ag[:, b], ve[:, b], stats_ready, aggr_ready, var_ready, b)
                    if b:
                        normalise(dve, X[:, (b - 1) * T:b * T], ag[:, b - 1], rstd[:, b - 1], rstd_ready, y[:, b - 1, :], y_ready, b - 1)

            @block.gpsimd
            def _(pool):
                pool.memset(minus_half[:, :], -0.5).then_inc(half_set, 1)
                pool.wait_ge(half_set, 1)
                for b in range(NB):
                    pool.wait_ge(var_ready, b + 1)
                    pool.tensor_tensor(rstd[:, b, :], ve[:, b, :], minus_half[:, :], ALU.pow).then_inc(rstd_ready, 1)

            @block.sync
            def _(sp):
                sp.dma_start(x0[:, :, :], X0.rearrange("p (b t) -> p b t", b=NB)).then_inc(x0_loaded, 16)
                for b in range(NB):
                    sp.wait_ge(y_ready, b + 1)
                    sp.dma_start(out[:, b * MT:(b + 1) * MT, :], y[:, b, :].rearrange("p (n d) -> p n d", d=D)).then_inc(stored, 16)
                sp.wait_ge(stored, 16 * NB)


def build(nc, dram, out):
    with ExitStack() as ctx:
        X = ctx.enter_context(nc.sbuf_tensor("X", [P, NB * T], F32))
        ident = ctx.enter_context(nc.sbuf_tensor("ident", [P, P], F32))
        banks = [ctx.enter_context(nc.psum_tensor(f"bank{i}", [P, 512], F32)) for i in range(8)]
        X0 = nc.dram_tensor("x0_kept", (P, NB * T), F32).ap()
        ident_loaded = ctx.enter_context(nc.semaphore("ident_loaded"))
        with nc.Block() as block:

            @block.sync
            def _(sp):
                sp.dma_start(ident[:, :], dram["ident"]).then_inc(ident_loaded, 16)
                sp.wait_ge(ident_loaded, 16)

        first_attention(nc, dram, X, ident, banks)
        with ExitStack() as inner:
            w = Weights(nc, inner)
            A = attention_buffers(nc, inner)
            attention_constants(nc, dram, inner, A, ident)
            SA, sa = semaphores(nc, inner, "a_", ATTENTION_SEMS)
            SF, sf = semaphores(nc, inner, "d_", FEED_FORWARD_SEMS)
            kept = inner.enter_context(nc.semaphore("kept"))
            with nc.Block() as block:

                @block.sync
                def _(sp):
                    for dst, src in w.attention_loads(dram, DEPTH - 1):
                        sp.dma_start(dst, src).then_inc(SF["weights"], 16)
                    sp.dma_start(X0, X[:, :]).then_inc(kept, 16)
                    sp.wait_ge(kept, 16)

                @block.scalar
                def _(act):
                    act.wait_ge(SF["weights"], 48)
                    split_attention_weights(A, w, SF, act=act)

                @block.vector
                def _(dve):
                    dve.wait_ge(SF["weights"], 48)
                    split_attention_weights(A, w, SF, dve=dve)

            clear(nc, sf)
            with nc.Fori(0, DEPTH) as layer:
                windowed_attention(nc, X, ident, banks, A, w, dram, layer, SA)
                clear(nc, sa)
                feed_forward(nc, dram, X, ident, banks, A, w, layer, SF)
                clear(nc, sf)
        last_norm(nc, X, X0, out)


def tables():
    f = np.float32
    i, j = np.arange(P)[:, None], np.arange(P)[None]
    q, k = np.arange(P)[:, None] % 64, np.arange(KW)[None]
    seen = (q <= k) & (k <= q + WIN)
    windows = np.stack([np.concatenate([seen & (k >= WIN)] + [seen] * 3, 1), np.concatenate([seen] * 4, 1)], 1)
    half = np.arange(0, DH, 2, dtype=f)
    inv = f(1) / f(10000.0) ** (half / f(DH))
    t = np.arange(T, dtype=f)
    freqs = np.concatenate([t[:, None] * inv[None]] * 2, 1)
    base = (half + f(0.4 * DH)) / f(1.4 * DH)
    scale = base[None] ** ((t - f(T // 2)) / f(WIN // 2))[:, None]
    scale = np.concatenate([scale] * 2, 1)
    sign = np.where(np.arange(DH) < DH // 2, f(-1), f(1))
    both = lambda x: np.stack([x * scale * f(8.0), x * (f(1) / scale)], 1).reshape(MT, P, 2, DH).transpose(1, 0, 2, 3)
    return {"ident": np.eye(P, dtype=f), "causal": np.where(i >= j, 0, NEG).astype(f),
            "windows": np.where(windows, 0, NEG).astype(f), "rot_cos": both(np.cos(freqs)).astype(f),
            "rot_sin": both(np.sin(freqs) * sign).astype(f)}


def kernel(**inputs):
    import concourse.bacc as bacc
    from concourse.bass_utils import run_bass_kernel_spmd

    x = {n: np.asarray(a) for n, a in inputs.items()}
    f = "L0_ffn_"
    qkv = x[f + "Wqkv"].reshape(DEPTH, D, 3, G, CQ).transpose(0, 1, 3, 2, 4).reshape(DEPTH, D, G, 3 * CQ)
    wo = x[f + "Wo"].reshape(DEPTH, 8, P, D).transpose(0, 2, 1, 3)
    scales = np.stack([x[f + "q_scale"], x[f + "k_scale"]], 1)
    w2 = np.zeros((DEPTH, NF * P, D), np.float32)
    w2[:, :DI] = x[f + "W2"]
    cols = np.zeros((DEPTH, P, 2 + 2 * NF), np.float32)
    cols[:, :, 0], cols[:, :, 1] = x[f + "ln_g"], x[f + "ln_b"]
    for c, (o, n) in enumerate(FCH):
        cols[:, :n, 2 + 2 * c] = x[f + "b1"][:, DI + o:DI + o + n]
        cols[:, :n, 3 + 2 * c] = x[f + "b1"][:, o:o + n]
    arrays = {
        "x": x["L0_attn_x"].reshape(NB * MT, P, D).transpose(1, 0, 2),
        "pqt": x["L0_attn_P_q"].transpose(2, 0, 1).reshape(DH, H * D),
        "pkt": x["L0_attn_P_k"].transpose(2, 0, 1).reshape(DH, H * D),
        "pv": x["L0_attn_P_v"].transpose(1, 0, 2).reshape(D, H * DH),
        "po": x["L0_attn_P_o"].transpose(0, 2, 1).reshape(8, P, D).transpose(1, 0, 2),
        "qkv": np.roll(qkv, -1, 0), "wo": np.roll(wo, -1, 0), "scales": np.roll(scales, -1, 0),
        "w1": x[f + "W1"], "w2": w2.reshape(DEPTH, NF, P, D).transpose(0, 2, 1, 3), "cols": cols, "b2": x[f + "b2"],
        **tables(),
    }
    arrays = {"in_" + n: np.ascontiguousarray(a) for n, a in arrays.items()}
    nc = bacc.Bacc("TRN2", target_bir_lowering=False, num_devices=1)
    dram = {n[3:]: nc.dram_tensor(n, a.shape, F32, kind="ExternalInput").ap() for n, a in arrays.items()}
    out = nc.dram_tensor("out", (P, NB * MT, D), F32, kind="ExternalOutput").ap()
    build(nc, dram, out)
    r = run_bass_kernel_spmd(nc, [arrays], core_ids=[0])
    got = np.asarray(r.results[0]["out"])
    return np.ascontiguousarray(got.transpose(1, 0, 2)).reshape(NB, T, D)
```

```python
from contextlib import ExitStack

import numpy as np
import concourse.bass as bass
from concourse import mybir

F32 = mybir.dt.float32
F32R = mybir.dt.float32r
BF16 = mybir.dt.bfloat16
ALU = mybir.AluOpType
ACT = mybir.ActivationFunctionType
AX = mybir.AxisListType

NB = 8
T = 512
D = 128
P = 128
MT = T // P
H = 16
DH = 64
DEPTH = 6
WIN = 32
G = 4
HG = H // G
CQ = HG * DH
WP = T // (2 * WIN)
KW = 3 * WIN
XC = WIN + T
DI = int(D * 4 * 2 / 3)
FCH = [(o, min(P, DI - o)) for o in range(0, DI, P)]
NF = len(FCH)
STEPS = H
NEG = -1e30
LN_EPS = 1e-5


def ge(engine, sem, count):
    if isinstance(count, int) and count <= 0:
        return
    engine.wait_ge(sem, count)


class At:

    def __init__(self, b, c):
        self.k = b * STEPS + c
        self.pos = c % STEPS
        self.batch = b + c // STEPS
        self.group = b * G + c // HG
        self.g, self.m = self.pos // MT, self.pos % MT
        self.par, self.gpar = self.pos % 2, self.g % 2


def at(b, j, lag):
    c = j - lag
    if isinstance(b, int) and not 0 <= b * STEPS + c < NB * STEPS:
        return None
    return At(b, c)


def every_step(engine, step, drain):
    for b in range(2):
        for j in range(STEPS):
            step(b, j, b)
    with engine.Fori(1, NB // 2) as i:
        for odd in range(2):
            for j in range(STEPS):
                step(i * 2 + odd, j, odd)
    for j in range(drain):
        step(NB, j, 0)


def tokens(X, batch):
    return X[:, batch * T:(batch + 1) * T] if isinstance(batch, int) else X[:, bass.ts(batch, T)]


F_XT, F_LOGITS, F_DIAGONAL, F_PROB = 14, 1, 2, 2


def first_attention(nc, dram, X, ident, banks):
    with ExitStack() as ctx:
        sb = lambda name, shape, dt=F32: ctx.enter_context(nc.sbuf_tensor("f_" + name, shape, dt))
        sem = lambda name: ctx.enter_context(nc.semaphore("f_" + name))
        pq_sb, pk_sb = sb("pq_sb", [DH, H * D]), sb("pk_sb", [DH, H * D])
        pv_sb = sb("pv_sb", [P, H * DH])
        po_sb = sb("po_sb", [P, 8, D])
        mh, ml = sb("mh", [P, H, D], F32R), sb("ml", [P, H, D], F32R)
        pvh, pvl = sb("pvh", [P, H * DH], F32R), sb("pvl", [P, H * DH], F32R)
        x_cur = sb("x_cur", [P, T])
        xh, xl = sb("xh", [P, 2, T], F32R), sb("xl", [P, 2, T], F32R)
        yh, yl = sb("yh", [P, 2, T], F32R), sb("yl", [P, 2, T], F32R)
        E = sb("E", [P, 2, MT, T])
        diag_only = sb("diag_only", [P, MT, P])
        ident_b, mask_b, mask_f = sb("ident_b", [P, P], BF16), sb("mask_b", [P, P], BF16), sb("mask_f", [P, P])
        negmax, esum = sb("negmax", [P, 2, MT]), sb("esum", [P, 4, MT])
        ediag, erec = sb("ediag", [P, 2, MT]), sb("erec", [P, 2, MT])
        prob, prob_all = sb("prob", [P, MT, H]), sb("prob_all", [P, MT, H])
        V = sb("V", [P, MT, H * DH])
        O = sb("O", [P, 2, T])
        OT = sb("OT", [P, 2, MT, P])
        xn = sb("xn", [P, T])
        st, ag = sb("st", [P, MT, 6]), sb("ag", [P, MT, 2])
        ve, rstd, mhalf = sb("ve", [P, MT]), sb("rstd", [P, MT]), sb("mhalf", [P, MT])
        p_y, p_s, p_v, p_t, p_z = banks[0], banks[1:5], banks[5], banks[6], banks[7]

        loaded, m_made, w_hi, w_lo, masks_made = (sem(n) for n in ("loaded", "m_made", "w_hi", "w_lo", "masks_made"))
        xc_ready, xt_ready, xh_ready, xl_ready = (sem(n) for n in ("xc_ready", "xt_ready", "xh_ready", "xl_ready"))
        y_ready, yh_ready, yl_ready = (sem(n) for n in ("y_ready", "yh_ready", "yl_ready"))
        logits_ready, max_ready, exp_ready = (sem(n) for n in ("logits_ready", "max_ready", "exp_ready"))
        diag_ready, rec_ready, prob_ready, all_ready = (sem(n) for n in ("diag_ready", "rec_ready", "prob_ready", "all_ready"))
        v_ready, v_out, o_ready, ot_ready, ot_out, z_ready = (sem(n) for n in ("v_ready", "v_out", "o_ready", "ot_ready", "ot_out", "z_ready"))
        sum_ready, stats_ready, aggr_ready, var_ready, rstd_ready, x_out = (sem(n) for n in ("sum_ready", "stats_ready", "aggr_ready", "var_ready", "rstd_ready", "x_out"))
        half_set = sem("half_set")

        with nc.Block() as block:

            @block.sync
            def _(sp):
                for dst, src in ((X[:, :].rearrange("p (n d) -> p n d", d=D), dram["x"]), (pq_sb[:, :], dram["pqt"]),
                                 (pk_sb[:, :], dram["pkt"]), (pv_sb[:, :], dram["pv"]),
                                 (po_sb[:, :, :], dram["po"]), (mask_f[:, :], dram["causal"])):
                    sp.dma_start(dst, src).then_inc(loaded, 16)
                sp.wait_ge(loaded, 96)
                with sp.Fori(1, NB) as b:
                    sp.wait_ge(xt_ready, b)
                    sp.dma_start(x_cur[:, :], tokens(X, b)).then_inc(xc_ready, 16)
                sp.wait_ge(xt_ready, NB)
                sp.dma_start(x_cur[:, :], tokens(X, NB - 1)).then_inc(xc_ready, 16)

            @block.tensor
            def _(pe):
                pe.wait_ge(loaded, 96)
                for q in range(4):
                    for h in range(4 * q, 4 * q + 4):
                        ins = pe.matmul(p_s[q][:, h % 4 * P:(h % 4 + 1) * P], pq_sb[:, h * D:(h + 1) * D],
                                        pk_sb[:, h * D:(h + 1) * D], start=True, stop=True)
                    ins.then_inc(m_made, 1)

                def transpose_x(b):
                    ge(pe, xc_ready, b * 16)
                    x = X if isinstance(b, int) and b == 0 else x_cur
                    for i in range(MT):
                        ins = pe.transpose(p_t[:, i * P:(i + 1) * P], x[:, i * P:(i + 1) * P], ident[:, :])
                    ins.then_inc(xt_ready, 1)

                transpose_x(0)
                pe.wait_ge(w_lo, 5)
                pe.wait_ge(masks_made, 2)

                def step(b, j, odd):
                    a = at(b, j, 0)

                    def next_x():
                        if a and j == F_XT:
                            ge(pe, ot_out, b * 8)
                            transpose_x(b + 1)

                    s_odd = lambda s: odd if s.pos <= j else 1 - odd

                    def logits():
                        s = at(b, j, F_LOGITS)
                        if s:
                            pe.wait_ge(yl_ready, s.k + 1)
                            for i in range(MT):
                                ge(pe, exp_ready, (s.k - 1) * MT + i + 1)
                                w, q = max(2 * P, (i + 1) * P), slice(i * P, (i + 1) * P)
                                pe.matmul(p_s[i][:, 0:w], yh[:, s.par, q], xh[:, s_odd(s), 0:w], start=True, stop=False)
                                pe.matmul(p_s[i][:, 0:w], yl[:, s.par, q], xh[:, s_odd(s), 0:w], start=False, stop=False)
                                pe.matmul(p_s[i][:, 0:w], yh[:, s.par, q], xl[:, s_odd(s), 0:w], start=False, stop=True)
                                pe.matmul(p_s[i][:, q], ident_b[:, :], mask_b[:, :], start=False, stop=True,
                                          skip_group_check=True).then_inc(logits_ready, 1)

                    def projected():
                        if a:
                            if j == 0:
                                pe.wait_ge(xl_ready, b + 1)
                            ge(pe, yl_ready, a.k)
                            pe.matmul(p_y[:, :], mh[:, a.pos, :], xh[:, odd, :], start=True, stop=False)
                            pe.matmul(p_y[:, :], ml[:, a.pos, :], xh[:, odd, :], start=False, stop=False)
                            pe.matmul(p_y[:, :], mh[:, a.pos, :], xl[:, odd, :], start=False, stop=True).then_inc(y_ready, 1)

                    def values():
                        if a and j >= 8:
                            i, half = divmod(j - 8, 2)
                            ge(pe, v_out, b * 8 + j - 8)
                            q, c = slice(i * P, (i + 1) * P), slice(half * T, half * T + T)
                            pe.matmul(p_v[:, :], xh[:, odd, q], pvh[:, c], start=True, stop=False)
                            pe.matmul(p_v[:, :], xl[:, odd, q], pvh[:, c], start=False, stop=False)
                            pe.matmul(p_v[:, :], xh[:, odd, q], pvl[:, c], start=False, stop=True).then_inc(v_ready, 1)

                    def out_projection():
                        o = at(b, j, STEPS)
                        if o and 5 <= j < 13:
                            i, half = divmod(j - 5, 2)
                            pe.wait_ge(ot_out, o.batch * 8 + j - 4)
                            if j == 5:
                                ge(pe, sum_ready, o.batch)
                            for c in range(4):
                                ins = pe.matmul(p_z[:, i * P:(i + 1) * P], OT[:, half, c, :], po_sb[:, 4 * half + c, :],
                                                start=(half + c == 0), stop=(half == 1 and c == 3))
                            ins.then_inc(z_ready, 1)

                    def transposes():
                        o = at(b, j, STEPS)
                        if o and 4 <= j < 12:
                            pe.wait_ge(o_ready, o.batch * 8 + j - 3)
                            ge(pe, ot_out, o.batch * 8 + j - 4)
                            if j == 4:
                                pe.wait_ge(xl_ready, o.batch + 2)
                            for c in range(4):
                                ins = pe.transpose(p_t[:, c * P:(c + 1) * P], O[:, j % 2, c * P:(c + 1) * P], ident[:, :])
                            ins.then_inc(ot_ready, 1)


                    for stage in (next_x, projected, logits, values, transposes, out_projection):
                        stage()

                every_step(pe, step, STEPS)

            @block.scalar
            def _(act):
                act.wait_ge(loaded, 96)
                for q in range(4):
                    act.wait_ge(m_made, q + 1)
                    act.activation(mh[:, 4 * q:4 * q + 4, :], p_s[q][:, :].rearrange("p (a b) -> p a b", a=4),
                                   ACT.Copy, scale=8.0).then_inc(w_hi, 1)
                act.activation(pvh[:, :], pv_sb[:, :], ACT.Copy).then_inc(w_hi, 1)

                def high_x(b, odd):
                    act.wait_ge(xt_ready, b + 1)
                    act.activation(xh[:, odd, :], p_t[:, :], ACT.Copy).then_inc(xh_ready, 1)

                high_x(0, 0)

                def step(b, j, odd):
                    a = at(b, j, 0)
                    if a and j == F_XT:
                        high_x(b + 1, 1 - odd)
                    def high_y():
                        if a:
                            act.wait_ge(y_ready, a.k + 1)
                            ge(act, logits_ready, (a.k - 1) * MT)
                            act.activation(yh[:, a.par, :], p_y[:, :], ACT.Copy).then_inc(yh_ready, 1)

                    def exps():
                        s = at(b, j, F_LOGITS)
                        if s:
                            for i in range(MT):
                                act.wait_ge(max_ready, s.k * MT + i + 1)
                                ge(act, diag_ready, (s.k - 2) * MT + i + 1)
                                if i == 0:
                                    ge(act, rec_ready, s.k - 3)
                                w = (i + 1) * P
                                act.activation(E[:, s.par, i, 0:w], p_s[i][:, 0:w], ACT.Exp, bias=negmax[:, s.par, i:i + 1],
                                               accum_out=esum[:, s.pos % 4, i:i + 1]).then_inc(exp_ready, 1)

                    def values():
                        if a and j >= 8:
                            i, half = divmod(j - 8, 2)
                            act.wait_ge(v_ready, b * 8 + j - 7)
                            ge(act, o_ready, (b - 1) * 8 + j - 7)
                            act.activation(V[:, i, half * T:half * T + T], p_v[:, :], ACT.Copy).then_inc(v_out, 1)

                    def transposed():
                        o = at(b, j, STEPS)
                        if o and 4 <= j < 12:
                            act.wait_ge(ot_ready, o.batch * 8 + j - 3)
                            ge(act, z_ready, o.batch * 8 + j - 5)
                            act.activation(OT[:, j % 2, :, :], p_t[:, :].rearrange("p (c t) -> p c t", c=4),
                                           ACT.Copy).then_inc(ot_out, 1)


                    for stage in (high_y, exps, transposed, values):
                        stage()

                every_step(act, step, STEPS)

            @block.gpsimd
            def _(pool):
                pool.memset(mhalf[:, :], -0.5).then_inc(half_set, 1)
                pool.wait_ge(half_set, 1)

                def step(b, j, odd):
                    o = at(b, j, STEPS)
                    if o and 3 <= j < 11:
                        i, half = divmod(j - 3, 2)
                        pool.wait_ge(v_out, o.batch * 8 + j - 2)
                        pool.wait_ge(all_ready, o.batch + 1)
                        ge(pool, ot_ready, o.batch * 8 + j - 4)
                        heads = prob_all[:, i, 8 * half:8 * half + 8].unsqueeze(2).to_broadcast([P, 8, DH])
                        pool.tensor_tensor(O[:, half, :].rearrange("p (h f) -> p h f", f=DH),
                                           V[:, i, half * T:half * T + T].rearrange("p (h f) -> p h f", f=DH),
                                           heads, ALU.mult).then_inc(o_ready, 1)
                    if o and j == 13:
                        pool.wait_ge(var_ready, o.batch + 1)
                        pool.tensor_tensor(rstd[:, :], ve[:, :], mhalf[:, :], ALU.pow).then_inc(rstd_ready, 1)

                every_step(pool, step, STEPS)

            @block.vector
            def _(dve):
                dve.wait_ge(loaded, 96)
                dve.tensor_copy(mask_b[:, :], mask_f[:, :]).then_inc(masks_made, 1)
                dve.tensor_copy(ident_b[:, :], ident[:, :]).then_inc(masks_made, 1)
                for q in range(4):
                    dve.wait_ge(w_hi, q + 1)
                    dve.scalar_tensor_tensor(ml[:, 4 * q:4 * q + 4, :].rearrange("p a b -> p (a b)"), p_s[q][:, :], 8.0,
                                             mh[:, 4 * q:4 * q + 4, :].rearrange("p a b -> p (a b)").bitcast(F32),
                                             ALU.mult, ALU.subtract).then_inc(w_lo, 1)
                dve.wait_ge(w_hi, 5)
                dve.tensor_tensor(pvl[:, :], pv_sb[:, :], pvh[:, :].bitcast(F32), ALU.subtract).then_inc(w_lo, 1)

                def low_x(b, odd):
                    dve.wait_ge(xh_ready, b + 1)
                    dve.tensor_tensor(xl[:, odd, :], p_t[:, :], xh[:, odd, :].bitcast(F32), ALU.subtract).then_inc(xl_ready, 1)

                low_x(0, 0)

                def step(b, j, odd):
                    a = at(b, j, 0)
                    if a and j == F_XT:
                        low_x(b + 1, 1 - odd)
                    def low_y():
                        if a:
                            dve.wait_ge(yh_ready, a.k + 1)
                            dve.tensor_tensor(yl[:, a.par, :], p_y[:, :], yh[:, a.par, :].bitcast(F32),
                                              ALU.subtract).then_inc(yl_ready, 1)

                    def diagonals():
                        g = at(b, j, F_DIAGONAL)
                        if g:
                            for i in range(MT):
                                dve.wait_ge(exp_ready, g.k * MT + i + 1)
                                if i == 0:
                                    ge(dve, prob_ready, g.k - 1)
                                ge(dve, diag_ready, (g.k - 1) * MT + i + 1)
                                dve.scalar_tensor_tensor(diag_only[:, i, :], E[:, g.par, i, i * P:(i + 1) * P], 1.0, ident[:, :], ALU.mult,
                                                         ALU.mult, accum_out=ediag[:, g.par, i:i + 1]).then_inc(diag_ready, 1)

                    def maxima():
                        s = at(b, j, F_LOGITS)
                        if s:
                            for i in range(MT):
                                dve.wait_ge(logits_ready, s.k * MT + i + 1)
                                if i == 0:
                                    ge(dve, exp_ready, (s.k - 1) * MT)
                                dve.tensor_reduce(negmax[:, s.par, i:i + 1], p_s[i][:, 0:(i + 1) * P], AX.X, ALU.max,
                                                  negate=True).then_inc(max_ready, 1)

                    def probs():
                        r = at(b, j, F_PROB)
                        if r:
                            dve.reciprocal(erec[:, r.par, :], esum[:, r.pos % 4, :]).then_inc(rec_ready, 1)
                            dve.wait_ge(rec_ready, r.k + 1)
                            dve.wait_ge(diag_ready, (r.k + 1) * MT)
                            dve.tensor_tensor(prob[:, :, r.pos], ediag[:, r.par, :], erec[:, r.par, :],
                                              ALU.mult).then_inc(prob_ready, 1)
                            if r.pos == H - 1:
                                dve.wait_ge(prob_ready, r.k + 1)
                                ge(dve, o_ready, r.batch * 8)
                                dve.tensor_copy(prob_all[:, :, :], prob[:, :, :]).then_inc(all_ready, 1)

                    def norms():
                        o = at(b, j, STEPS)
                        if o and j == 13:
                            dve.wait_ge(z_ready, (o.batch + 1) * 8)
                            ge(dve, x_out, o.batch)
                            dve.tensor_tensor(xn[:, :], tokens(X, o.batch), p_z[:, :], ALU.add).then_inc(sum_ready, 1)
                            dve.wait_ge(sum_ready, o.batch + 1)
                            statistics(dve, xn, st, ag, ve, stats_ready, aggr_ready, var_ready, o.batch)
                        if o and j == 14:
                            normalise(dve, xn, ag, rstd, rstd_ready, tokens(X, o.batch), x_out, o.batch)


                    for stage in (diagonals, low_y, maxima, norms, probs):
                        stage()

                every_step(dve, step, STEPS)


def statistics(dve, x, st, ag, ve, stats_ready, aggr_ready, var_ready, n):
    for i in range(MT):
        ins = dve.bn_stats(st[:, i, :], x[:, i * D:(i + 1) * D])
    ins.then_inc(stats_ready, 1)
    dve.wait_ge(stats_ready, n + 1)
    dve.memset(ve[:, :], 0.0)
    for i in range(MT):
        ins = dve.bn_aggr(ag[:, i, :], st[:, i, :])
    ins.then_inc(aggr_ready, 1)
    dve.wait_ge(aggr_ready, n + 1)
    dve.tensor_scalar(ve[:, :], ag[:, :, 1], LN_EPS, None, ALU.add).then_inc(var_ready, 1)


def normalise(dve, x, ag, rstd, rstd_ready, out, done, n):
    dve.wait_ge(rstd_ready, n + 1)
    for i in range(MT):
        ins = dve.tensor_scalar(out[:, i * D:(i + 1) * D], x[:, i * D:(i + 1) * D], ag[:, i, 0:1], rstd[:, i:i + 1],
                                ALU.subtract, ALU.mult)
    ins.then_inc(done, 1)


class Weights:

    def __init__(self, nc, ctx):
        sb = lambda name, shape: ctx.enter_context(nc.sbuf_tensor(name, shape, F32))
        self.qkv = sb("w_qkv", [P, G, 3 * CQ])
        self.scales = sb("w_scales", [P, 2, DH])
        self.out = sb("w_out", [P, 8, D])
        self.w1 = sb("w_w1", [P, 2 * DI])
        self.w2 = sb("w_w2", [P, NF, D])
        self.cols = sb("w_cols", [P, 2 + 2 * NF])
        self.b2 = sb("w_b2", [P, D])

    def attention_loads(self, dram, layer):
        return ((self.qkv[:, :, :], dram["qkv"][layer]),
                (self.scales[:, :, :], dram["scales"][layer].partition_broadcast(P)))

    def feed_forward_loads(self, dram, layer):
        return ((self.w1[:, :], dram["w1"][layer]), (self.w2[:, :, :], dram["w2"][layer]),
                (self.cols[:, :], dram["cols"][layer]), (self.b2[:, :], dram["b2"][layer].partition_broadcast(P)))


XT_STEP = 5
LAG_R, LAG_A, LAG_T, LAG_S, LAG_E, LAG_PT, LAG_O, LAG_Y = 1, 2, 3, 7, 8, 10, 11, 15


def attention_buffers(nc, ctx):
    made = {}

    def sb(name, shape, dt=F32):
        made[name] = ctx.enter_context(nc.sbuf_tensor("a_" + name, shape, dt))

    for n in ("wh", "wl"):
        sb(n, [P, G, 3 * CQ], F32R)
    for n in ("tabs_c", "tabs_s", "rot_c", "rot_s"):
        sb(n, [P, MT, 2, DH])
    sb("masks_f", [P, 2, 4 * KW])
    sb("masks", [P, 2, 4 * KW], F32R)
    sb("ident_r", [P, P], F32R)
    sb("minus_half", [P, 2 * HG])
    sb("first_exp", [P, 1])
    sb("x_cur", [P, T])
    sb("xs", [P, T])
    for n in ("xh", "xl"):
        sb(n, [P, 2, XC], F32R)
    sb("sq", [P, 2 * CQ])
    for n in ("ssq", "ssqc", "rn"):
        sb(n, [P, 2, 2 * HG])
    for n in ("qn", "u", "v", "r"):
        sb(n, [P, 2, 2 * CQ])
    sb("QT", [P, 2, 2, WP, P])
    sb("KT", [P, 2, 2, XC])
    sb("V", [KW, G, WP, CQ])
    sb("E", [P, 2, 4, KW])
    sb("PN", [P, 2, 4, KW])
    for n in ("negmax", "esum", "erec"):
        sb(n, [P, 2, 4])
    sb("PT", [KW, 2, 4, P])
    sb("OT", [P, 2, 2, T])
    return made


def attention_constants(nc, dram, ctx, A, ident):
    sem = lambda name: ctx.enter_context(nc.semaphore("c_" + name))
    loaded, zeroed, made = sem("loaded"), sem("zeroed"), sem("made")
    with nc.Block() as block:

        @block.sync
        def _(sp):
            for dst, src in ((A["tabs_c"][:, :, :, :], "rot_cos"), (A["tabs_s"][:, :, :, :], "rot_sin"),
                             (A["masks_f"][:, :, :], "windows")):
                sp.dma_start(dst, dram[src]).then_inc(loaded, 16)

        @block.gpsimd
        def _(pool):
            pool.memset(A["minus_half"][:, :], -0.5).then_inc(zeroed, 1)
            pool.memset(A["QT"][:, :, :, :, :], 0.0).then_inc(zeroed, 1)
            pool.memset(A["KT"][:, :, :, 0:WIN], 0.0).then_inc(zeroed, 1)
            pool.wait_ge(zeroed, 3)

        @block.vector
        def _(dve):
            for n in ("xh", "xl"):
                dve.memset(A[n][:, :, 0:WIN + 2].bitcast(F32), 0.0).then_inc(made, 1)
            dve.tensor_copy(A["ident_r"][:, :], ident[:, :]).then_inc(made, 1)
            dve.wait_ge(loaded, 48)
            dve.tensor_copy(A["masks"][:, :, :], A["masks_f"][:, :, :]).then_inc(made, 1)
            dve.wait_ge(made, 4)


def split_attention_weights(A, w, S, groups, act=None, dve=None):
    for g in range(*groups):
        if act:
            act.activation(A["wh"][:, g, :], w.qkv[:, g, :], ACT.Copy).then_inc(S["aw_hi"], 1)
        if dve:
            dve.wait_ge(S["aw_hi"], g + 1)
            dve.tensor_tensor(A["wl"][:, g, :], w.qkv[:, g, :], A["wh"][:, g, :].bitcast(F32), ALU.subtract)
    if dve and groups[1] == G:
        rot_c, rot_s, tabs_c, tabs_s = A["rot_c"], A["rot_s"], A["tabs_c"], A["tabs_s"]
        dve.tensor_tensor(rot_c[:, :, :, :].rearrange("p m s f -> p m (s f)"),
                          tabs_c[:, :, :, :].rearrange("p m s f -> p m (s f)"),
                          w.scales[:, :, :].rearrange("p s f -> p (s f)").unsqueeze(1).to_broadcast([P, MT, 2 * DH]),
                          ALU.mult)
        swap = lambda x: x.rearrange("p s (h f) -> p s h f", h=2)
        for m in range(MT):
            dve.tensor_tensor(swap(rot_s[:, m, :, :]), swap(tabs_s[:, m, :, :]), swap(w.scales[:, :, :])[:, :, ::-1, :],
                              ALU.mult)


def windowed_attention(nc, X, ident, banks, A, w, dram, layer, S):
    wh, wl, rot_c, rot_s, masks, ident_r, minus_half = (
        A[n] for n in ("wh", "wl", "rot_c", "rot_s", "masks", "ident_r", "minus_half"))
    x_cur, xs, xh, xl, sq, ssq, ssqc, rn, qn, u, v, r = (
        A[n] for n in ("x_cur", "xs", "xh", "xl", "sq", "ssq", "ssqc", "rn", "qn", "u", "v", "r"))
    QT, KT, V, E, PN, negmax, esum, erec, PT, OT = (
        A[n] for n in ("QT", "KT", "V", "E", "PN", "negmax", "esum", "erec", "PT", "OT"))
    p_qk, p_v, p_t, p_s, p_p, p_o, p_y = banks[0:2], banks[2], banks[3], banks[4], banks[5], banks[6], banks[7]
    with nc.Block() as block:

        @block.sync
        def _(sp):
            for dst, src in w.feed_forward_loads(dram, layer) + w.attention_loads(dram, layer):
                sp.dma_start(dst, src).then_inc(S["weights"], 16)
            with sp.Fori(1, NB) as b:
                sp.wait_ge(S["xt"], b)
                sp.dma_start(x_cur[:, :], tokens(X, b)).then_inc(S["xc"], 16)
            sp.wait_ge(S["xt"], NB)
            sp.dma_start(x_cur[:, :], tokens(X, NB - 1)).then_inc(S["xc"], 16)
            sp.wait_ge(S["weights"], 96)

        @block.tensor
        def _(pe):
            def transpose_x(b):
                ge(pe, S["xc"], b * 16)
                x = X if isinstance(b, int) and b == 0 else x_cur
                for i in range(MT):
                    ins = pe.transpose(p_v[:, i * P:(i + 1) * P], x[:, i * P:(i + 1) * P], ident[:, :])
                ins.then_inc(S["xt"], 1)

            def step(b, j, odd):
                a = at(b, j, 0)

                def next_x():
                    if a and j == XT_STEP:
                        ge(pe, S["v_out"], a.k)
                        transpose_x(b + 1)

                def project():
                    if a:
                        if j == 0:
                            pe.wait_ge(S["xl"], b + 1)
                        ge(pe, S["sq"], a.k - 1)
                        ge(pe, S["qn"], a.k - 1)
                        m, g = slice(WIN + a.m * P, WIN + (a.m + 1) * P), a.g
                        pe.matmul(p_qk[a.par][:, :], xh[:, odd, m], wh[:, g, 0:2 * CQ], start=True, stop=False)
                        pe.matmul(p_qk[a.par][:, :], xl[:, odd, m], wh[:, g, 0:2 * CQ], start=False, stop=False)
                        pe.matmul(p_qk[a.par][:, :], xh[:, odd, m], wl[:, g, 0:2 * CQ], start=False, stop=True).then_inc(S["qk"], 1)

                def values():
                    if a:
                        g = a.g
                        ge(pe, S["v_out"], a.k)
                        if j in (0, XT_STEP):
                            pe.wait_ge(S["xs"], b + 1 + (j > 0))
                        c = slice(2 * CQ, 3 * CQ)
                        for n in range(1 + (a.m == MT - 1)):
                            m = slice((a.m + n) * P, (a.m + n) * P + (WIN if n else P))
                            to = p_v[0:WIN if n else P, n * CQ:(n + 1) * CQ]
                            pe.matmul(to, xh[:, odd, m], wh[:, g, c], start=True, stop=False)
                            pe.matmul(to, xl[:, odd, m], wh[:, g, c], start=False, stop=False)
                            ins = pe.matmul(to, xh[:, odd, m], wl[:, g, c], start=False, stop=True)
                        ins.then_inc(S["v"], 1)

                def outputs():
                    o = at(b, j, LAG_O)
                    if o:
                        pe.wait_ge(S["pt_out"], o.k + 1)
                        pe.wait_ge(S["v_out"], o.k - o.m + 4)
                        ge(pe, S["o_out"], o.k)
                        hp, half = divmod(o.m, 2)
                        for n in range(4):
                            ins = pe.matmul(p_o[:, n * P:(n + 1) * P], V[:, o.g, 4 * half + n, hp * P:(hp + 1) * P],
                                            PT[:, o.par, n, :], start=True, stop=True)
                        ins.then_inc(S["o"], 1)

                def output_projection():
                    y = at(b, j, LAG_Y)
                    if y:
                        pe.wait_ge(S["o_out"], y.k - y.m + 4)
                        if y.pos == 0:
                            ge(pe, S["x_out"], y.batch)
                        i = y.m
                        for hp in range(2):
                            ins = pe.matmul(p_y[:, i * P:(i + 1) * P], OT[:, y.gpar, hp, i * P:(i + 1) * P],
                                            w.out[:, 2 * y.g + hp, :], start=(y.pos + hp == 0),
                                            stop=(y.g == G - 1 and hp == 1), skip_group_check=True)
                        ins.then_inc(S["y"], 1)

                def transpose_probs():
                    t = at(b, j, LAG_PT)
                    if t:
                        pe.wait_ge(S["pn"], t.k + 1)
                        ge(pe, S["pt_out"], t.k)
                        for n in range(4):
                            ins = pe.transpose(p_p[0:KW, n * P:(n + 1) * P], PN[:, t.par, n, :], ident[:, :])
                        ins.then_inc(S["pt"], 1)

                def transpose_qk():
                    t = at(b, j, LAG_T)
                    if t:
                        pe.wait_ge(S["r"], t.k + 1)
                        ge(pe, S["k_out"], t.k)
                        ge(pe, S["q_out"], t.k)
                        for c in range(4):
                            ins = pe.transpose(p_t[:, c * P:(c + 1) * P], r[:, t.par, c * P:(c + 1) * P], ident[:, :])
                        ins.then_inc(S["qkt"], 1)

                def logits():
                    s = at(b, j, LAG_S)
                    if s:
                        pe.wait_ge(S["k_out"], s.k - s.m + 4)
                        pe.wait_ge(S["q_out"], s.k - s.m + 4)
                        ge(pe, S["exp"], s.k)
                        hp, half = divmod(s.m, 2)
                        pe.matmul(p_s[:, 0:4 * KW], ident_r[:, :], masks[:, int(half > 0), :], start=True, stop=True)
                        for n in range(4):
                            first = 64 * (4 * half + n)
                            ins = pe.matmul(p_s[:, n * KW:(n + 1) * KW], QT[:, s.gpar, hp, 4 * half + n, :],
                                            KT[:, s.gpar, hp, first:first + KW], start=False, stop=True,
                                            skip_group_check=True)
                        ins.then_inc(S["logits"], 1)

                for stage in (project, next_x, outputs, transpose_probs, transpose_qk, values, logits, output_projection):
                    stage()

            transpose_x(0)
            every_step(pe, step, LAG_Y + 1)

        @block.scalar
        def _(act):
            def shift_x(b):
                act.wait_ge(S["xt"], b + 1)
                ge(act, S["xl"], b)
                act.activation(xs[0:64, :], p_v[0:64, :], ACT.Copy)
                act.activation(xs[64:P, 1:T], p_v[64:P, 0:T - 1], ACT.Copy).then_inc(S["xs"], 1)

            act.activation(A["first_exp"][:, :], minus_half[:, 0:1], ACT.Exp)
            act.wait_ge(S["x_pad"], 1)
            shift_x(0)

            def step(b, j, odd):
                a = at(b, j, 0)

                def next_x():
                    if a and j == XT_STEP:
                        shift_x(b + 1)

                def values():
                    v_ = at(b, j, 1)
                    if v_:
                        act.wait_ge(S["v"], v_.k + 1)
                        ge(act, S["o"], v_.k - v_.m - 12)
                        pair = 2 * v_.m
                        act.activation(V[:, v_.g, pair, :], p_v[0:KW, 0:CQ], ACT.Copy)
                        if v_.m:
                            act.activation(V[64:KW, v_.g, pair - 1, :], p_v[0:WIN, 0:CQ], ACT.Copy)
                        if v_.m == MT - 1:
                            act.activation(V[64:KW, v_.g, pair + 1, :], p_v[0:WIN, CQ:], ACT.Copy)
                        act.activation(V[0:64, v_.g, pair + 1, :], p_v[64:P, 0:CQ], ACT.Copy).then_inc(S["v_out"], 1)

                def squares():
                    if a:
                        act.wait_ge(S["qk"], a.k + 1)
                        ge(act, S["summed"], a.k)
                        act.activation(sq[:, :], p_qk[a.par][:, :], ACT.Square).then_inc(S["sq"], 1)

                def exps():
                    s = at(b, j, LAG_E)
                    if s:
                        act.wait_ge(S["max"], s.k + 1)
                        ge(act, S["pn"], s.k - 1)
                        for n in range(4):
                            ins = act.activation(E[:, s.par, n, :], p_s[:, n * KW:(n + 1) * KW], ACT.Exp,
                                                 bias=negmax[:, s.par, n:n + 1], accum_out=esum[:, s.par, n:n + 1])
                        ins.then_inc(S["exp"], 1)

                def outputs():
                    o = at(b, j, LAG_O)
                    if o:
                        act.wait_ge(S["o"], o.k + 1)
                        ge(act, S["y"], o.k - o.m - 4)
                        hp, half = divmod(o.m, 2)
                        for h in range(2):
                            q = slice(64 * h, 64 * h + 64)
                            ins = act.activation(
                                OT[q, o.gpar, hp, 4 * 64 * half:4 * 64 * (half + 1)].rearrange("p (n t) -> p n t", n=4),
                                p_o[q, :].rearrange("p (n h t) -> p n h t", n=4, h=2)[:, :, h, :], ACT.Copy)
                        ins.then_inc(S["o_out"], 1)

                def probs():
                    t = at(b, j, LAG_PT)
                    if t:
                        act.wait_ge(S["pt"], t.k + 1)
                        ge(act, S["o"], t.k - 1)
                        act.activation(PT[:, t.par, :, :], p_p[0:KW, :].rearrange("p (n q) -> p n q", n=4),
                                       ACT.Copy).then_inc(S["pt_out"], 1)

                def keys():
                    t = at(b, j, LAG_T)
                    if t:
                        act.wait_ge(S["qkt"], t.k + 1)
                        ge(act, S["logits"], t.k - t.m - 4)
                        c = WIN + t.m * P
                        act.activation(KT[:, t.gpar, :, c:c + P], p_t[:, 2 * P:].rearrange("p (h t) -> p h t", h=2),
                                       ACT.Copy).then_inc(S["k_out"], 1)


                for stage in (values, exps, next_x, squares, keys, outputs, probs):
                    stage()

            every_step(act, step, LAG_Y + 1)

        @block.gpsimd
        def _(pool):
            def step(b, j, odd):
                def rotate():
                    a = at(b, j, LAG_R)
                    if a:
                        pool.wait_ge(S["qn"], a.k + 1)
                        ge(pool, S["r"], a.k - 1)
                        view = lambda x: x[:, a.par, :].rearrange("p (s h f) -> p s h f", s=2, h=HG)
                        tab = rot_c[:, a.m, :, :].unsqueeze(2).to_broadcast([P, 2, HG, DH])
                        pool.tensor_tensor(view(u), view(qn), tab, ALU.mult).then_inc(S["u"], 1)

                def power():
                    a = at(b, j, 0)
                    if a:
                        pool.wait_ge(S["red"], a.k + 1)
                        ge(pool, S["qn"], a.k - 1)
                        pool.tensor_tensor(rn[:, a.par, :], ssqc[:, a.par, :], minus_half[:, :], ALU.pow).then_inc(S["rn"], 1)

                def probs():
                    s = at(b, j, LAG_E)
                    if s:
                        pool.wait_ge(S["rec"], s.k + 1)
                        ge(pool, S["pt"], s.k - 1)
                        pool.tensor_tensor(PN[:, s.par, :, :], E[:, s.par, :, :],
                                           erec[:, s.par, :].unsqueeze(2).to_broadcast([P, 4, KW]),
                                           ALU.mult).then_inc(S["pn"], 1)


                for stage in (rotate, power, probs):
                    stage()

            every_step(pool, step, LAG_Y + 1)

        @block.vector
        def _(dve):
            def split_x(b, odd):
                dve.wait_ge(S["xs"], b + 1)
                dve.tensor_copy(xh[:, odd, WIN:XC], xs[:, :]).then_inc(S["xh"], 1)
                dve.wait_ge(S["xh"], b + 1)
                dve.tensor_tensor(xl[:, odd, WIN:XC], xs[:, :], xh[:, odd, WIN:XC].bitcast(F32),
                                  ALU.subtract).then_inc(S["xl"], 1)

            dve.memset(xs[:, 0:1], 0.0).then_inc(S["x_pad"], 1)
            split_x(0, 0)

            def step(b, j, odd):
                a = at(b, j, 0)

                def next_x():
                    if a and j == XT_STEP + 1:
                        split_x(b + 1, 1 - odd)

                def maxima():
                    s = at(b, j, LAG_E)
                    if s:
                        dve.wait_ge(S["logits"], s.k + 1)
                        ge(dve, S["exp"], s.k - 1)
                        dve.tensor_reduce(negmax[:, s.par, :], p_s[:, 0:4 * KW].rearrange("p (n k) -> p n k", n=4), AX.X,
                                          ALU.max, negate=True).then_inc(S["max"], 1)

                def add():
                    c = at(b, j, LAG_A)
                    if c:
                        dve.wait_ge(S["u"], c.k + 1)
                        dve.wait_ge(S["v_rot"], c.k + 1)
                        ge(dve, S["qkt"], c.k - 1)
                        dve.tensor_tensor(r[:, c.par, :], u[:, c.par, :], v[:, c.par, :], ALU.add).then_inc(S["r"], 1)

                def units():
                    c = at(b, j, LAG_R)
                    if c:
                        dve.wait_ge(S["rn"], c.k + 1)
                        ge(dve, S["u"], c.k - 1)
                        ge(dve, S["v_rot"], c.k - 1)
                        heads = lambda x: x.rearrange("p (h f) -> p h f", f=DH)
                        dve.tensor_tensor(heads(qn[:, c.par, :]), heads(p_qk[c.par][:, :]),
                                          rn[:, c.par, :].unsqueeze(2).to_broadcast([P, 2 * HG, DH]),
                                          ALU.mult).then_inc(S["qn"], 1)

                def sines():
                    c = at(b, j, LAG_R)
                    if c:
                        dve.wait_ge(S["qn"], c.k + 1)
                        ge(dve, S["v_rot"], c.k - 1)
                        ge(dve, S["r"], c.k - 1)
                        halves = lambda x: x.rearrange("p (s h t f) -> p s h t f", s=2, h=HG, t=2)
                        tab = rot_s[:, c.m, :, :].rearrange("p s (t f) -> p s t f", t=2).unsqueeze(2).to_broadcast([P, 2, HG, 2, DH // 2])
                        dve.tensor_tensor(halves(v[:, c.par, :]), halves(qn[:, c.par, :])[:, :, :, ::-1, :], tab,
                                          ALU.mult).then_inc(S["v_rot"], 1)

                def norms():
                    if a:
                        dve.wait_ge(S["sq"], a.k + 1)
                        ge(dve, S["red"], a.k - 1)
                        dve.tensor_reduce(ssq[:, a.par, :], sq[:, :].rearrange("p (h f) -> p h f", f=DH), AX.X,
                                          ALU.add).then_inc(S["summed"], 1)
                        dve.wait_ge(S["summed"], a.k + 1)
                        ge(dve, S["rn"], a.k - 1)
                        dve.tensor_scalar(ssqc[:, a.par, :], ssq[:, a.par, :], 1e-24, None, ALU.max).then_inc(S["red"], 1)

                def queries():
                    t = at(b, j, LAG_T)
                    if t:
                        dve.wait_ge(S["k_out"], t.k + 1)
                        ge(dve, S["logits"], t.k - t.m - 4)
                        for h in range(2):
                            q = slice(64 * h, 64 * h + 64)
                            ins = dve.tensor_copy(QT[q, t.gpar, :, 2 * t.m:2 * t.m + 2, q],
                                                  p_t[q, 0:2 * P].rearrange("p (h w t) -> p h w t", h=2, w=2))
                        ins.then_inc(S["q_out"], 1)

                def reciprocals():
                    s = at(b, j, LAG_E)
                    if s:
                        dve.wait_ge(S["exp"], s.k + 1)
                        ge(dve, S["pn"], s.k - 1)
                        dve.reciprocal(erec[:, s.par, :], esum[:, s.par, :]).then_inc(S["rec"], 1)

                def residual():
                    y = at(b, j, LAG_Y)
                    if y and y.pos == STEPS - 1:
                        dve.wait_ge(S["y"], y.k + 1)
                        dve.tensor_tensor(tokens(X, y.batch), tokens(X, y.batch), p_y[:, :], ALU.add).then_inc(S["x_out"], 1)


                for stage in (maxima, add, units, sines, reciprocals, norms, queries, next_x, residual):
                    stage()

            every_step(dve, step, LAG_Y + 1)


ATTENTION_SEMS = ("x_pad xs xc weights xt xh xl k_out q_out pt_out v_out o_out o y pn pt exp "
                  "logits r qkt sq qn qk v max red u rec rn v_rot summed x_out").split()


def semaphores(nc, ctx, prefix, names):
    made = {n: ctx.enter_context(nc.semaphore(prefix + n)) for n in names}
    return made, list(made.values())


def clear(nc, sems):
    for s in sems:
        nc.sync.sem_clear(s)
    nc.all_engine_barrier()


def feed_forward(nc, dram, X, ident, banks, A, w, layer, S):
    with ExitStack() as ctx:
        sb = lambda name, shape, dt=F32: ctx.enter_context(nc.sbuf_tensor("d_" + name, shape, dt))
        w1h, w1l = sb("w1h", [P, 2 * DI], F32R), sb("w1l", [P, 2 * DI], F32R)
        minus_half = sb("minus_half", [P, MT])
        x_cur, y = A["x_cur"], A["sq"]
        xs, xn = A["v"][:, 0, :], A["r"][:, 0, :]
        st, ag = sb("st", [P, MT, 6]), sb("ag", [P, MT, 2])
        ve, rstd = sb("ve", [P, MT]), sb("rstd", [P, MT])
        xt, xh, xl = sb("xt", [P, T]), sb("xh", [P, T], F32R), sb("xl", [P, T], F32R)
        gate, h = sb("gate", [P, NF, T]), sb("h", [P, NF, T])
        p_x, p_n, p_h, p_y = banks[0], banks[1], banks[2:6], banks[7]
        p_r = banks[6]

        def every_batch(engine, step):
            for n in range(4):
                step(n)
            with engine.Fori(4, NB) as n:
                step(n)
            for n in range(NB, NB + 3):
                step(n)

        def run_stages(n, stages):
            for stage, lag in stages:
                if not isinstance(n, int) or 0 <= n - lag < NB:
                    stage(n - lag)

        with nc.Block() as block:

            @block.sync
            def _(sp):
                sp.dma_start(w.out[:, :, :], dram["wo"][layer]).then_inc(S["weights"], 16)
                with sp.Fori(1, NB) as b:
                    sp.wait_ge(S["xt"], b)
                    sp.dma_start(x_cur[:, :], tokens(X, b)).then_inc(S["xc"], 16)
                sp.wait_ge(S["weights"], 16)

            @block.tensor
            def _(pe):
                def transpose_x(b):
                    ge(pe, S["xc"], b * 16)
                    ge(pe, S["xs"], b)
                    x = X if isinstance(b, int) and b == 0 else x_cur
                    for i in range(MT):
                        ins = pe.transpose(p_x[:, i * P:(i + 1) * P], x[:, i * P:(i + 1) * P], ident[:, :])
                    ins.then_inc(S["xt"], 1)

                def back(b):
                    pe.wait_ge(S["xs"], b + 1)
                    ge(pe, S["normed"], b)
                    for i in range(MT):
                        ins = pe.transpose(p_n[:, i * P:(i + 1) * P], xs[:, i * P:(i + 1) * P], ident[:, :])
                    ins.then_inc(S["back"], 1)

                def again(b):
                    pe.wait_ge(S["normed"], b + 1)
                    ge(pe, S["affine"], b)
                    for i in range(MT):
                        ins = pe.transpose(p_r[:, i * P:(i + 1) * P], xn[:, i * P:(i + 1) * P], ident[:, :])
                    ins.then_inc(S["again"], 1)

                def up(b):
                    pe.wait_ge(S["xl"], b + 1)
                    if isinstance(b, int) and b == 0:
                        pe.wait_ge(S["w_lo"], 1)
                    for c, (o, n) in enumerate(FCH):
                        for part in range(2):
                            bank = p_h[2 * (c % 2) + part]
                            if c >= 2:
                                pe.wait_ge(S["h"] if part else S["gate"], NF * b + c - 1)
                            col = slice(DI * (1 - part) + o, DI * (1 - part) + o + n)
                            pe.matmul(bank[0:n, :], w1h[:, col], xh[:, :], start=True, stop=False)
                            pe.matmul(bank[0:n, :], w1l[:, col], xh[:, :], start=False, stop=False)
                            pe.matmul(bank[0:n, :], w1h[:, col], xl[:, :], start=False, stop=True).then_inc(S["up"], 1)

                def down(b):
                    ge(pe, S["x_out"], b)
                    for c, (o, n) in enumerate(FCH):
                        pe.wait_ge(S["h"], b * NF + c + 1)
                        for i in range(MT):
                            ins = pe.matmul(p_y[:, i * P:(i + 1) * P], h[0:n, c, i * P:(i + 1) * P], w.w2[0:n, c, :],
                                            start=(c + i == 0), stop=(c == NF - 1), skip_group_check=True)
                    ins.then_inc(S["down"], 1)

                def step(n):
                    run_stages(n, ((transpose_x, 0), (up, 3), (back, 1), (again, 2), (down, 3)))

                every_batch(pe, step)

            @block.scalar
            def _(act):
                def shift(b):
                    act.wait_ge(S["xt"], b + 1)
                    ge(act, S["back"], b)
                    act.activation(xs[0:64, :], p_x[0:64, :], ACT.Copy)
                    act.activation(xs[64:P, 1:T], p_x[64:P, 0:T - 1], ACT.Copy).then_inc(S["xs"], 1)

                def gates(b):
                    for c, (o, n) in enumerate(FCH):
                        act.wait_ge(S["up"], b * 2 * NF + 2 * c + 1)
                        act.activation(gate[0:n, c, :], p_h[2 * (c % 2)][0:n, :], ACT.Gelu,
                                       bias=w.cols[0:n, 2 + 2 * c:3 + 2 * c]).then_inc(S["gate"], 1)

                def affine(b):
                    act.wait_ge(S["again"], b + 1)
                    ge(act, S["xl"], b)
                    act.activation(xt[:, :], p_r[:, :], ACT.Identity, scale=w.cols[:, 0:1],
                                   bias=w.cols[:, 1:2]).then_inc(S["affine"], 1)

                def step(n):
                    run_stages(n, ((gates, 3), (affine, 2), (shift, 0)))
                    if isinstance(n, int) and n < 2:
                        split_attention_weights(A, w, S, (2 * n, 2 * n + 2), act=act)

                act.activation(w1h[:, :], w.w1[:, :], ACT.Copy).then_inc(S["w_hi"], 1)
                act.wait_ge(S["pads"], 1)
                every_batch(act, step)

            @block.gpsimd
            def _(pool):
                pool.memset(minus_half[:, :], -0.5).then_inc(S["const_made"], 1)
                pool.wait_ge(S["const_made"], 1)

                def power(b):
                    pool.wait_ge(S["var"], b + 1)
                    pool.tensor_tensor(rstd[:, :], ve[:, :], minus_half[:, :], ALU.pow).then_inc(S["rstd"], 1)

                power(0)
                with pool.Fori(1, NB) as b:
                    power(b)

            @block.vector
            def _(dve):
                def products(b):
                    for c, (o, n) in enumerate(FCH):
                        dve.wait_ge(S["up"], b * 2 * NF + 2 * c + 2)
                        dve.wait_ge(S["gate"], b * NF + c + 1)
                        ge(dve, S["down"], b)
                        dve.scalar_tensor_tensor(h[0:n, c, :], p_h[2 * (c % 2) + 1][0:n, :],
                                                 w.cols[0:n, 3 + 2 * c:4 + 2 * c], gate[0:n, c, :], ALU.add,
                                                 ALU.mult).then_inc(S["h"], 1)

                def stats(b):
                    dve.wait_ge(S["back"], b + 1)
                    ge(dve, S["normed"], b)
                    statistics(dve, p_n, st, ag, ve, S["stats"], S["aggr"], S["var"], b)

                def split(b):
                    dve.wait_ge(S["affine"], b + 1)
                    ge(dve, S["up"], b * 2 * NF)
                    dve.tensor_copy(xh[:, :], xt[:, :]).then_inc(S["xh"], 1)
                    dve.wait_ge(S["xh"], b + 1)
                    dve.tensor_tensor(xl[:, :], xt[:, :], xh[:, :].bitcast(F32), ALU.subtract).then_inc(S["xl"], 1)

                def residual(b):
                    dve.wait_ge(S["down"], b + 1)
                    dve.tensor_tensor(y[:, :].rearrange("p (i d) -> p i d", d=D), p_y[:, :].rearrange("p (i d) -> p i d", d=D),
                                      w.b2[:, :].unsqueeze(1).to_broadcast([P, MT, D]), ALU.add).then_inc(S["x_out"], 1)
                    dve.wait_ge(S["x_out"], b + 1)
                    dve.tensor_tensor(tokens(X, b), tokens(X, b), y[:, :], ALU.add).then_inc(S["x_added"], 1)

                def norm(b):
                    ge(dve, S["again"], b)
                    normalise(dve, p_n, ag, rstd, S["rstd"], xn[:, :], S["normed"], b)

                def step(n):
                    run_stages(n, ((products, 3), (stats, 1), (split, 2), (residual, 3), (norm, 1)))
                    if isinstance(n, int) and n < 4:
                        split_attention_weights(A, w, S, (n, n + 1), dve=dve)

                dve.memset(xs[:, 0:1], 0.0).then_inc(S["pads"], 1)
                dve.wait_ge(S["w_hi"], 1)
                dve.tensor_tensor(w1l[:, :], w.w1[:, :], w1h[:, :].bitcast(F32), ALU.subtract).then_inc(S["w_lo"], 1)
                every_batch(dve, step)


FEED_FORWARD_SEMS = ("aw_hi weights xc xt xs back normed again affine xl xh gate h up down w_hi w_lo pads const_made var rstd "
                     "stats aggr x_out x_added").split()


def last_norm(nc, X, X0, out):
    with ExitStack() as ctx:
        sb = lambda name, shape: ctx.enter_context(nc.sbuf_tensor("n_" + name, shape, F32))
        sem = lambda name: ctx.enter_context(nc.semaphore("n_" + name))
        y, x0 = sb("y", [P, NB, T]), sb("x0", [P, NB, T])
        x0_loaded, sum_ready = sem("x0_loaded"), sem("sum_ready")
        st, ag = sb("st", [P, NB, MT, 6]), sb("ag", [P, NB, MT, 2])
        ve, rstd, minus_half = sb("ve", [P, NB, MT]), sb("rstd", [P, NB, MT]), sb("minus_half", [P, MT])
        stats_ready, aggr_ready, var_ready, rstd_ready, y_ready, half_set, stored = (
            sem(n) for n in ("stats_ready", "aggr_ready", "var_ready", "rstd_ready", "y_ready", "half_set", "stored"))
        with nc.Block() as block:

            @block.vector
            def _(dve):
                for b in range(NB + 1):
                    if b < NB:
                        dve.wait_ge(x0_loaded, 16)
                        dve.tensor_tensor(X[:, b * T:(b + 1) * T], X[:, b * T:(b + 1) * T], x0[:, b, :],
                                          ALU.add).then_inc(sum_ready, 1)
                        dve.wait_ge(sum_ready, b + 1)
                        statistics(dve, X[:, b * T:(b + 1) * T], st[:, b], ag[:, b], ve[:, b], stats_ready, aggr_ready, var_ready, b)
                    if b:
                        normalise(dve, X[:, (b - 1) * T:b * T], ag[:, b - 1], rstd[:, b - 1], rstd_ready, y[:, b - 1, :], y_ready, b - 1)

            @block.gpsimd
            def _(pool):
                pool.memset(minus_half[:, :], -0.5).then_inc(half_set, 1)
                pool.wait_ge(half_set, 1)
                for b in range(NB):
                    pool.wait_ge(var_ready, b + 1)
                    pool.tensor_tensor(rstd[:, b, :], ve[:, b, :], minus_half[:, :], ALU.pow).then_inc(rstd_ready, 1)

            @block.sync
            def _(sp):
                sp.dma_start(x0[:, :, :], X0.rearrange("p (b t) -> p b t", b=NB)).then_inc(x0_loaded, 16)
                for b in range(NB):
                    sp.wait_ge(y_ready, b + 1)
                    sp.dma_start(out[:, b * MT:(b + 1) * MT, :], y[:, b, :].rearrange("p (n d) -> p n d", d=D)).then_inc(stored, 16)
                sp.wait_ge(stored, 16 * NB)


def build(nc, dram, out):
    with ExitStack() as ctx:
        X = ctx.enter_context(nc.sbuf_tensor("X", [P, NB * T], F32))
        ident = ctx.enter_context(nc.sbuf_tensor("ident", [P, P], F32))
        banks = [ctx.enter_context(nc.psum_tensor(f"bank{i}", [P, 512], F32)) for i in range(8)]
        X0 = nc.dram_tensor("x0_kept", (P, NB * T), F32).ap()
        ident_loaded = ctx.enter_context(nc.semaphore("ident_loaded"))
        with nc.Block() as block:

            @block.sync
            def _(sp):
                sp.dma_start(ident[:, :], dram["ident"]).then_inc(ident_loaded, 16)
                sp.wait_ge(ident_loaded, 16)

        first_attention(nc, dram, X, ident, banks)
        with ExitStack() as inner:
            w = Weights(nc, inner)
            A = attention_buffers(nc, inner)
            attention_constants(nc, dram, inner, A, ident)
            SA, sa = semaphores(nc, inner, "a_", ATTENTION_SEMS)
            SF, sf = semaphores(nc, inner, "d_", FEED_FORWARD_SEMS)
            kept = inner.enter_context(nc.semaphore("kept"))
            with nc.Block() as block:

                @block.sync
                def _(sp):
                    for dst, src in w.attention_loads(dram, DEPTH - 1) + ((w.out[:, :, :], dram["wo"][DEPTH - 1]),):
                        sp.dma_start(dst, src).then_inc(SF["weights"], 16)
                    sp.dma_start(X0, X[:, :]).then_inc(kept, 16)
                    sp.wait_ge(kept, 16)

                @block.scalar
                def _(act):
                    act.wait_ge(SF["weights"], 48)
                    split_attention_weights(A, w, SF, (0, G), act=act)

                @block.vector
                def _(dve):
                    dve.wait_ge(SF["weights"], 48)
                    split_attention_weights(A, w, SF, (0, G), dve=dve)

            clear(nc, sf)
            with nc.Fori(0, DEPTH) as layer:
                windowed_attention(nc, X, ident, banks, A, w, dram, layer, SA)
                clear(nc, sa)
                feed_forward(nc, dram, X, ident, banks, A, w, layer, SF)
                clear(nc, sf)
        last_norm(nc, X, X0, out)


def tables():
    f = np.float32
    i, j = np.arange(P)[:, None], np.arange(P)[None]
    q, k = np.arange(P)[:, None] % 64, np.arange(KW)[None]
    seen = (q <= k) & (k <= q + WIN)
    windows = np.stack([np.concatenate([seen & (k >= WIN)] + [seen] * 3, 1), np.concatenate([seen] * 4, 1)], 1)
    half = np.arange(0, DH, 2, dtype=f)
    inv = f(1) / f(10000.0) ** (half / f(DH))
    t = np.arange(T, dtype=f)
    freqs = np.concatenate([t[:, None] * inv[None]] * 2, 1)
    base = (half + f(0.4 * DH)) / f(1.4 * DH)
    scale = base[None] ** ((t - f(T // 2)) / f(WIN // 2))[:, None]
    scale = np.concatenate([scale] * 2, 1)
    sign = np.where(np.arange(DH) < DH // 2, f(-1), f(1))
    both = lambda x: np.stack([x * scale * f(8.0), x * (f(1) / scale)], 1).reshape(MT, P, 2, DH).transpose(1, 0, 2, 3)
    return {"ident": np.eye(P, dtype=f), "causal": np.where(i >= j, 0, NEG).astype(f),
            "windows": np.where(windows, 0, NEG).astype(f), "rot_cos": both(np.cos(freqs)).astype(f),
            "rot_sin": both(np.sin(freqs) * sign).astype(f)}


def kernel(**inputs):
    import concourse.bacc as bacc
    from concourse.bass_utils import run_bass_kernel_spmd

    x = {n: np.asarray(a) for n, a in inputs.items()}
    f = "L0_ffn_"
    qkv = x[f + "Wqkv"].reshape(DEPTH, D, 3, G, CQ).transpose(0, 1, 3, 2, 4).reshape(DEPTH, D, G, 3 * CQ)
    wo = x[f + "Wo"].reshape(DEPTH, 8, P, D).transpose(0, 2, 1, 3)
    scales = np.stack([x[f + "q_scale"], x[f + "k_scale"]], 1)
    w2 = np.zeros((DEPTH, NF * P, D), np.float32)
    w2[:, :DI] = x[f + "W2"]
    cols = np.zeros((DEPTH, P, 2 + 2 * NF), np.float32)
    cols[:, :, 0], cols[:, :, 1] = x[f + "ln_g"], x[f + "ln_b"]
    for c, (o, n) in enumerate(FCH):
        cols[:, :n, 2 + 2 * c] = x[f + "b1"][:, DI + o:DI + o + n]
        cols[:, :n, 3 + 2 * c] = x[f + "b1"][:, o:o + n]
    arrays = {
        "x": x["L0_attn_x"].reshape(NB * MT, P, D).transpose(1, 0, 2),
        "pqt": x["L0_attn_P_q"].transpose(2, 0, 1).reshape(DH, H * D),
        "pkt": x["L0_attn_P_k"].transpose(2, 0, 1).reshape(DH, H * D),
        "pv": x["L0_attn_P_v"].transpose(1, 0, 2).reshape(D, H * DH),
        "po": x["L0_attn_P_o"].transpose(0, 2, 1).reshape(8, P, D).transpose(1, 0, 2),
        "qkv": np.roll(qkv, -1, 0), "wo": np.roll(wo, -1, 0), "scales": np.roll(scales, -1, 0),
        "w1": x[f + "W1"], "w2": w2.reshape(DEPTH, NF, P, D).transpose(0, 2, 1, 3), "cols": cols, "b2": x[f + "b2"],
        **tables(),
    }
    arrays = {"in_" + n: np.ascontiguousarray(a) for n, a in arrays.items()}
    nc = bacc.Bacc("TRN2", target_bir_lowering=False, num_devices=1)
    dram = {n[3:]: nc.dram_tensor(n, a.shape, F32, kind="ExternalInput").ap() for n, a in arrays.items()}
    out = nc.dram_tensor("out", (P, NB * MT, D), F32, kind="ExternalOutput").ap()
    build(nc, dram, out)
    r = run_bass_kernel_spmd(nc, [arrays], core_ids=[0])
    got = np.asarray(r.results[0]["out"])
    return np.ascontiguousarray(got.transpose(1, 0, 2)).reshape(NB, T, D)
```
